# Optimizing a Trainium2 kernel written in Bass

```python
import numpy as np
import jax
import jax.numpy as jnp

def _softmax(x, axis=-1):
    return jax.nn.softmax(x, axis=axis)

def _gelu(x):
    return jax.nn.gelu(x, approximate=True)

def _silu(x):
    return jax.nn.silu(x)

def _sigmoid(x):
    return jax.nn.sigmoid(x)

def _layernorm(x, axis=-1, eps=1e-05):
    m = jnp.mean(x, axis=axis, keepdims=True)
    v = jnp.var(x, axis=axis, keepdims=True)
    return (x - m) / jnp.sqrt(v + eps)

def _scatter_add(tgt, idx, src, axis=0):
    return tgt.at[idx].add(src)

def _segment_sum(src, seg, n):
    return jax.ops.segment_sum(src, seg, n)
kernel_name = 'mk_dlrm_tower_d1_rec_r8_cfec8c'

def setup_inputs(seed: int=0):
    np.random.seed(seed)
    _w = jnp.asarray

    def _rec_inputs():
        import jax
        import jax.numpy as jnp
        _tk = jax.random.key(seed)
        dense_ctx = jax.random.normal(jax.random.fold_in(_tk, 190), (1024, 16), jnp.float32)
        ids = jnp.stack([jax.random.randint(jax.random.fold_in(_tk, 200 + f), (1024,), 0, v, jnp.int32) for f, v in enumerate([12500, 12500, 12500, 12500, 125000, 1000, 1000, 12500, 125000, 125000, 1250, 1000, 1250, 125000, 1000, 1000, 1250, 1000, 1000, 125000, 1250, 1250, 1250, 1250, 1000, 125000, 1250, 125000, 1250, 1250, 12500, 1000])], axis=1)
        tbl_0 = 0.05 * jax.random.normal(jax.random.fold_in(_tk, 500 + 0), (12500, 16), jnp.float32)
        tbl_1 = 0.05 * jax.random.normal(jax.random.fold_in(_tk, 500 + 1), (12500, 16), jnp.float32)
        tbl_2 = 0.05 * jax.random.normal(jax.random.fold_in(_tk, 500 + 2), (12500, 16), jnp.float32)
        tbl_3 = 0.05 * jax.random.normal(jax.random.fold_in(_tk, 500 + 3), (12500, 16), jnp.float32)
        tbl_4 = 0.05 * jax.random.normal(jax.random.fold_in(_tk, 500 + 4), (125000, 16), jnp.float32)
        tbl_5 = 0.05 * jax.random.normal(jax.random.fold_in(_tk, 500 + 5), (1000, 16), jnp.float32)
        tbl_6 = 0.05 * jax.random.normal(jax.random.fold_in(_tk, 500 + 6), (1000, 16), jnp.float32)
        tbl_7 = 0.05 * jax.random.normal(jax.random.fold_in(_tk, 500 + 7), (12500, 16), jnp.float32)
        tbl_8 = 0.05 * jax.random.normal(jax.random.fold_in(_tk, 500 + 8), (125000, 16), jnp.float32)
        tbl_9 = 0.05 * jax.random.normal(jax.random.fold_in(_tk, 500 + 9), (125000, 16), jnp.float32)
        tbl_10 = 0.05 * jax.random.normal(jax.random.fold_in(_tk, 500 + 10), (1250, 16), jnp.float32)
        tbl_11 = 0.05 * jax.random.normal(jax.random.fold_in(_tk, 500 + 11), (1000, 16), jnp.float32)
        tbl_12 = 0.05 * jax.random.normal(jax.random.fold_in(_tk, 500 + 12), (1250, 16), jnp.float32)
        tbl_13 = 0.05 * jax.random.normal(jax.random.fold_in(_tk, 500 + 13), (125000, 16), jnp.float32)
        tbl_14 = 0.05 * jax.random.normal(jax.random.fold_in(_tk, 500 + 14), (1000, 16), jnp.float32)
        tbl_15 = 0.05 * jax.random.normal(jax.random.fold_in(_tk, 500 + 15), (1000, 16), jnp.float32)
        tbl_16 = 0.05 * jax.random.normal(jax.random.fold_in(_tk, 500 + 16), (1250, 16), jnp.float32)
        tbl_17 = 0.05 * jax.random.normal(jax.random.fold_in(_tk, 500 + 17), (1000, 16), jnp.float32)
        tbl_18 = 0.05 * jax.random.normal(jax.random.fold_in(_tk, 500 + 18), (1000, 16), jnp.float32)
        tbl_19 = 0.05 * jax.random.normal(jax.random.fold_in(_tk, 500 + 19), (125000, 16), jnp.float32)
        tbl_20 = 0.05 * jax.random.normal(jax.random.fold_in(_tk, 500 + 20), (1250, 16), jnp.float32)
        tbl_21 = 0.05 * jax.random.normal(jax.random.fold_in(_tk, 500 + 21), (1250, 16), jnp.float32)
        tbl_22 = 0.05 * jax.random.normal(jax.random.fold_in(_tk, 500 + 22), (1250, 16), jnp.float32)
        tbl_23 = 0.05 * jax.random.normal(jax.random.fold_in(_tk, 500 + 23), (1250, 16), jnp.float32)
        tbl_24 = 0.05 * jax.random.normal(jax.random.fold_in(_tk, 500 + 24), (1000, 16), jnp.float32)
        tbl_25 = 0.05 * jax.random.normal(jax.random.fold_in(_tk, 500 + 25), (125000, 16), jnp.float32)
        tbl_26 = 0.05 * jax.random.normal(jax.random.fold_in(_tk, 500 + 26), (1250, 16), jnp.float32)
        tbl_27 = 0.05 * jax.random.normal(jax.random.fold_in(_tk, 500 + 27), (125000, 16), jnp.float32)
        tbl_28 = 0.05 * jax.random.normal(jax.random.fold_in(_tk, 500 + 28), (1250, 16), jnp.float32)
        tbl_29 = 0.05 * jax.random.normal(jax.random.fold_in(_tk, 500 + 29), (1250, 16), jnp.float32)
        tbl_30 = 0.05 * jax.random.normal(jax.random.fold_in(_tk, 500 + 30), (12500, 16), jnp.float32)
        tbl_31 = 0.05 * jax.random.normal(jax.random.fold_in(_tk, 500 + 31), (1000, 16), jnp.float32)
        _rk = jax.random.fold_in(_tk, 7)
        W_top1 = 0.0606339 * jax.random.normal(jax.random.fold_in(_tk, 801), (272, 512), jnp.float32)
        W_top2 = 0.0441942 * jax.random.normal(jax.random.fold_in(_tk, 802), (512, 256), jnp.float32)
        W_top3 = 0.0625 * jax.random.normal(jax.random.fold_in(_tk, 803), (256, 1), jnp.float32)
        b_top1 = jnp.zeros((512,), jnp.float32)
        b_top2 = jnp.zeros((256,), jnp.float32)
        return (dense_ctx, ids, tbl_0, tbl_1, tbl_2, tbl_3, tbl_4, tbl_5, tbl_6, tbl_7, tbl_8, tbl_9, tbl_10, tbl_11, tbl_12, tbl_13, tbl_14, tbl_15, tbl_16, tbl_17, tbl_18, tbl_19, tbl_20, tbl_21, tbl_22, tbl_23, tbl_24, tbl_25, tbl_26, tbl_27, tbl_28, tbl_29, tbl_30, tbl_31, W_top1, b_top1, W_top2, b_top2, W_top3)
    dense_ctx, ids, tbl_0, tbl_1, tbl_2, tbl_3, tbl_4, tbl_5, tbl_6, tbl_7, tbl_8, tbl_9, tbl_10, tbl_11, tbl_12, tbl_13, tbl_14, tbl_15, tbl_16, tbl_17, tbl_18, tbl_19, tbl_20, tbl_21, tbl_22, tbl_23, tbl_24, tbl_25, tbl_26, tbl_27, tbl_28, tbl_29, tbl_30, tbl_31, W_top1, b_top1, W_top2, b_top2, W_top3 = _rec_inputs()

    def _L0_rec_setup():
        import jax, jax.numpy as jnp
        import numpy as np
        NUM_FIELDS = 32
        EMBED_DIM = 16
        BATCH = 512
        CROSS_SIZES = [128, 128, 128]

        def _cin_forward(x, Ws, bs):
            x0 = x
            h = x
            xs = []
            n_layers = len(Ws)
            for i in range(n_layers):
                B, F, E = x0.shape
                G = h.shape[1]
                z = (x0[:, :, None, :] * h[:, None, :, :]).reshape(B, F * G, E)
                y = jax.nn.relu(jnp.einsum('oc,bce->boe', Ws[i], z) + bs[i][None, :, None])
                if i != n_layers - 1:
                    half = y.shape[1] // 2
                    x_keep, h = (y[:, :half, :], y[:, half:, :])
                else:
                    x_keep, h = (y, y)
                xs.append(x_keep)
            return jnp.sum(jnp.concatenate(xs, axis=1), axis=2)
        key = jax.random.key(seed)
        ks = jax.random.split(key, 8)
        x = jax.random.normal(ks[0], (BATCH, NUM_FIELDS, EMBED_DIM), dtype=jnp.float32)
        prev = NUM_FIELDS
        inp = {'x': x}
        for i, cs in enumerate(CROSS_SIZES):
            in_ch = NUM_FIELDS * prev
            scale = 1.0 / np.sqrt(in_ch)
            inp[f'W{i}'] = jax.random.uniform(ks[1 + 2 * i], (cs, in_ch), dtype=jnp.float32, minval=-scale, maxval=scale)
            inp[f'b{i}'] = jax.random.uniform(ks[2 + 2 * i], (cs,), dtype=jnp.float32, minval=-scale, maxval=scale)
            prev = cs // 2
        return inp
    _L0_rec_all = _L0_rec_setup()
    _L0_rec_in = {k: v for k, v in _L0_rec_all.items() if k in ('W0', 'b0', 'W1', 'b1', 'W2', 'b2')}
    del _L0_rec_all
    return {'dense_ctx': dense_ctx, 'ids': ids, 'tbl_0': tbl_0, 'tbl_1': tbl_1, 'tbl_2': tbl_2, 'tbl_3': tbl_3, 'tbl_4': tbl_4, 'tbl_5': tbl_5, 'tbl_6': tbl_6, 'tbl_7': tbl_7, 'tbl_8': tbl_8, 'tbl_9': tbl_9, 'tbl_10': tbl_10, 'tbl_11': tbl_11, 'tbl_12': tbl_12, 'tbl_13': tbl_13, 'tbl_14': tbl_14, 'tbl_15': tbl_15, 'tbl_16': tbl_16, 'tbl_17': tbl_17, 'tbl_18': tbl_18, 'tbl_19': tbl_19, 'tbl_20': tbl_20, 'tbl_21': tbl_21, 'tbl_22': tbl_22, 'tbl_23': tbl_23, 'tbl_24': tbl_24, 'tbl_25': tbl_25, 'tbl_26': tbl_26, 'tbl_27': tbl_27, 'tbl_28': tbl_28, 'tbl_29': tbl_29, 'tbl_30': tbl_30, 'tbl_31': tbl_31, 'W_top1': W_top1, 'b_top1': b_top1, 'W_top2': W_top2, 'b_top2': b_top2, 'W_top3': W_top3, 'L0_rec_W0': _L0_rec_in['W0'], 'L0_rec_b0': _L0_rec_in['b0'], 'L0_rec_W1': _L0_rec_in['W1'], 'L0_rec_b1': _L0_rec_in['b1'], 'L0_rec_W2': _L0_rec_in['W2'], 'L0_rec_b2': _L0_rec_in['b2']}

def reference(dense_ctx, ids, tbl_0, tbl_1, tbl_2, tbl_3, tbl_4, tbl_5, tbl_6, tbl_7, tbl_8, tbl_9, tbl_10, tbl_11, tbl_12, tbl_13, tbl_14, tbl_15, tbl_16, tbl_17, tbl_18, tbl_19, tbl_20, tbl_21, tbl_22, tbl_23, tbl_24, tbl_25, tbl_26, tbl_27, tbl_28, tbl_29, tbl_30, tbl_31, W_top1, b_top1, W_top2, b_top2, W_top3, L0_rec_W0, L0_rec_b0, L0_rec_W1, L0_rec_b1, L0_rec_W2, L0_rec_b2):
    import jax
    import jax.numpy as jnp

    def _L0_rec_ref(x, W0, b0, W1, b1, W2, b2):
        import jax, jax.numpy as jnp
        import numpy as np
        NUM_FIELDS = 32
        EMBED_DIM = 16
        BATCH = 512
        CROSS_SIZES = [128, 128, 128]

        def _cin_forward(x, Ws, bs):
            x0 = x
            h = x
            xs = []
            n_layers = len(Ws)
            for i in range(n_layers):
                B, F, E = x0.shape
                G = h.shape[1]
                z = (x0[:, :, None, :] * h[:, None, :, :]).reshape(B, F * G, E)
                y = jax.nn.relu(jnp.einsum('oc,bce->boe', Ws[i], z) + bs[i][None, :, None])
                if i != n_layers - 1:
                    half = y.shape[1] // 2
                    x_keep, h = (y[:, :half, :], y[:, half:, :])
                else:
                    x_keep, h = (y, y)
                xs.append(x_keep)
            return jnp.sum(jnp.concatenate(xs, axis=1), axis=2)
        return _cin_forward(x, [W0, W1, W2], [b0, b1, b2])
    e = jnp.stack([tbl_0[ids[:, 0]], tbl_1[ids[:, 1]], tbl_2[ids[:, 2]], tbl_3[ids[:, 3]], tbl_4[ids[:, 4]], tbl_5[ids[:, 5]], tbl_6[ids[:, 6]], tbl_7[ids[:, 7]], tbl_8[ids[:, 8]], tbl_9[ids[:, 9]], tbl_10[ids[:, 10]], tbl_11[ids[:, 11]], tbl_12[ids[:, 12]], tbl_13[ids[:, 13]], tbl_14[ids[:, 14]], tbl_15[ids[:, 15]], tbl_16[ids[:, 16]], tbl_17[ids[:, 17]], tbl_18[ids[:, 18]], tbl_19[ids[:, 19]], tbl_20[ids[:, 20]], tbl_21[ids[:, 21]], tbl_22[ids[:, 22]], tbl_23[ids[:, 23]], tbl_24[ids[:, 24]], tbl_25[ids[:, 25]], tbl_26[ids[:, 26]], tbl_27[ids[:, 27]], tbl_28[ids[:, 28]], tbl_29[ids[:, 29]], tbl_30[ids[:, 30]], tbl_31[ids[:, 31]]], axis=1)
    z = _L0_rec_ref(e, L0_rec_W0, L0_rec_b0, L0_rec_W1, L0_rec_b1, L0_rec_W2, L0_rec_b2)
    z = z.reshape(z.shape[0], -1)
    h = jnp.concatenate([z, dense_ctx], axis=1)
    h = jnp.maximum(h @ W_top1 + b_top1, 0.0)
    h = jnp.maximum(h @ W_top2 + b_top2, 0.0)
    y = h @ W_top3
    return y

_drawn_inputs = setup_inputs


def setup_inputs(seed=0):
    import zlib

    import numpy as np

    out = dict(_drawn_inputs(seed))
    spreads = {'b_top1': (0.0, 0.35), 'b_top2': (0.0, 0.397)}
    factors = {'tbl_0': 8.0,
     'tbl_1': 8.0,
     'tbl_2': 8.0,
     'tbl_3': 8.0,
     'tbl_4': 8.0,
     'tbl_5': 8.0,
     'tbl_6': 8.0,
     'tbl_7': 8.0,
     'tbl_8': 8.0,
     'tbl_9': 8.0,
     'tbl_10': 8.0,
     'tbl_11': 8.0,
     'tbl_12': 8.0,
     'tbl_13': 8.0,
     'tbl_14': 8.0,
     'tbl_15': 8.0,
     'tbl_16': 8.0,
     'tbl_17': 8.0,
     'tbl_18': 8.0,
     'tbl_19': 8.0,
     'tbl_20': 8.0,
     'tbl_21': 8.0,
     'tbl_22': 8.0,
     'tbl_23': 8.0,
     'tbl_24': 8.0,
     'tbl_25': 8.0,
     'tbl_26': 8.0,
     'tbl_27': 8.0,
     'tbl_28': 8.0,
     'tbl_29': 8.0,
     'tbl_30': 8.0,
     'tbl_31': 8.0,
     'L0_rec_W0': 8.0,
     'L0_rec_W1': 8.0,
     'L0_rec_W2': 8.0,
     'L0_rec_b0': 4.772,
     'L0_rec_b1': 6.923,
     'L0_rec_b2': 7.269}
    for name, (base, spread) in spreads.items():
        noise = np.random.default_rng([zlib.crc32(name.encode()), seed]).standard_normal(out[name].shape)
        drawn = base * np.exp(spread * noise) if base else spread * noise
        out[name] = jnp.asarray(drawn.astype(out[name].dtype))
    for name, factor in factors.items():
        out[name] = (out[name] * factor).astype(out[name].dtype)
    return out
```

```python
import concourse.bass as bass
from concourse import mybir
from contextlib import ExitStack

FIELDS = 32
EMBED = 16
BATCH = 1024
MAPS = 128
HALF = MAPS // 2
GROUPS = 4
SAMPLES = 32
CHUNKS = BATCH // SAMPLES
COLS = SAMPLES * EMBED
PER_GROUP = SAMPLES // GROUPS
TILES = FIELDS * HALF // 128
BLOCK = 4
BLOCKS = TILES // BLOCK
PAIR = 2
L0_PAIRS = 2
L12_PAIRS = TILES // PAIR
SHIFTS = [[0, 8, 12, 16], [8, 16, 20, 24], [4, 20, 24, 28], [12, 28, 0, 4]]
MID = BLOCK
MIDQ = FIELDS
MIDN = FIELDS // 2
ROWS = 2 * FIELDS
DENSE = 16
HID1, HID2 = 512, 256
ZRING = 4
TOP_LOADS = 7
PAIRS_PER_CHUNK = L0_PAIRS + 2 * L12_PAIRS


def shift(k, quarter):
    return SHIFTS[quarter][k // BLOCK] + k % BLOCK


def pair_z1(c, g):
    return L0_PAIRS + PAIRS_PER_CHUNK * c + g


def pair_z0(c, g):
    return g if isinstance(c, int) and c == 0 else pair_z1(c - 1, L12_PAIRS + g)


def pair_z2(c, g):
    late = 0 if isinstance(c, int) and c == CHUNKS - 1 else L0_PAIRS
    return pair_z1(c, L12_PAIRS + late + g)


def slot_z1(s, g):
    return (L0_PAIRS + PAIRS_PER_CHUNK * s + g) % ZRING


def slot_z0(c, s, g):
    return g if isinstance(c, int) and c == 0 else slot_z1(1 - s, L12_PAIRS + g)


def slot_z2(s, g, last):
    return slot_z1(s, L12_PAIRS + (0 if last else L0_PAIRS) + g)


def dlrm_tower(nc, tables, ids, field_base, dense_t, w0a, w0b, w0ma, w0mb, w1, w2,
               bias0, bias1, bias2, wt1, bt1, wt2, bt2, wt3, out):
    fp32 = mybir.dt.float32
    i32 = mybir.dt.int32
    ALU = mybir.AluOpType
    ACT = mybir.ActivationFunctionType
    AX = mybir.AxisListType

    ctx = ExitStack()
    with ctx:
        def sb(name, shape, dt=fp32):
            return ctx.enter_context(nc.sbuf_tensor(name, shape, dt))

        def sem(name):
            return ctx.enter_context(nc.semaphore(name))

        scratch = nc.dram_tensor("x_scratch", [CHUNKS, ROWS, COLS], fp32, kind="Internal")

        ids_sb = sb("ids_sb", [128, CHUNKS * PER_GROUP], i32)
        base_sb = sb("base_sb", [128, 1])
        rows_sb = sb("rows_sb", [128, CHUNKS * PER_GROUP], i32)
        rows_now = [sb(f"rows_now{s}", [128, PER_GROUP], i32) for s in range(2)]
        gathered = [sb(f"gathered{s}", [128, PER_GROUP * EMBED]) for s in range(2)]
        xsh = [sb(f"xsh{s}", [128, TILES, COLS]) for s in range(2)]
        xall = [sb(f"xall{s}", [128, COLS]) for s in range(2)]
        z = [sb(f"z{s}", [128, PAIR, COLS]) for s in range(ZRING)]
        zmid = sb("zmid", [128, COLS])
        h1 = sb("h1", [128, COLS])
        h2 = sb("h2", [128, COLS])
        kept01 = [sb(f"kept01{s}", [128, COLS]) for s in range(2)]
        kept2 = [sb(f"kept2{s}", [128, COLS]) for s in range(2)]
        pool01 = sb("pool01", [128, BATCH])
        pool2 = sb("pool2", [128, BATCH])
        w0a_sb = sb("w0a_sb", [128, BLOCK, MAPS])
        w0b_sb = sb("w0b_sb", [128, BLOCK, MAPS])
        w0ma_sb = sb("w0ma_sb", [128, MAPS])
        w0mb_sb = sb("w0mb_sb", [128, MAPS])
        w0 = sb("w0", [128, BLOCK, MAPS])
        w0m = sb("w0m", [128, MAPS])
        w1_sb = sb("w1_sb", [128, TILES, MAPS])
        w2_sb = sb("w2_sb", [128, TILES, MAPS])
        bias = [sb(f"bias{n}_sb", [128, 1]) for n in range(3)]
        wt1_sb = sb("wt1_sb", [128, 2, HID1])
        wt1d_sb = sb("wt1d_sb", [DENSE, HID1])
        dense_sb = sb("dense_sb", [DENSE, BATCH])
        bt1_sb = sb("bt1_sb", [128, HID1 // 128])
        wt2_sb = sb("wt2_sb", [128, HID1 // 128, HID2])
        bt2_sb = sb("bt2_sb", [128, HID2 // 128])
        wt3_sb = sb("wt3_sb", [128, HID2 // 128])
        hid1 = sb("hid1", [128, HID1 // 128, BATCH])
        hid2 = sb("hid2", [128, HID2 // 128, BATCH])
        y_sb = sb("y_sb", [1, BATCH])

        banks = [ctx.enter_context(nc.psum_tensor(f"bank{n}", [128, COLS], fp32)) for n in range(8)]
        y0, y1, y2 = banks[0:2], banks[2:4], banks[4:6]

        ids_loaded = sem("ids_loaded")
        rows_ready = sem("rows_ready")
        rows_staged = sem("rows_staged")
        gather_done = [sem(f"gather_done{s}") for s in range(2)]
        scratch_written = [sem(f"scratch_written{s}") for s in range(2)]
        xall_loaded = [sem(f"xall_loaded{s}") for s in range(2)]
        xsh_loaded = [[sem(f"xsh_loaded{s}_{b}") for b in range(BLOCKS)] for s in range(2)]
        w0_loaded = sem("w0_loaded")
        w1_loaded = sem("w1_loaded")
        w2_loaded = sem("w2_loaded")
        bias_loaded = sem("bias_loaded")
        top_loaded = sem("top_loaded")
        w0_ready = sem("w0_ready")
        pair_ready = sem("pair_ready")
        pair_used = sem("pair_used")
        mid_ready = sem("mid_ready")
        y0_ready = sem("y0_ready")
        h1_ready = sem("h1_ready")
        h2_ready = sem("h2_ready")
        kept0_ready = sem("kept0_ready")
        kept1_ready = sem("kept1_ready")
        kept2_ready = sem("kept2_ready")
        pooled01 = sem("pooled01")
        pooled2 = sem("pooled2")
        hid1_psum = sem("hid1_psum")
        hid1_ready = sem("hid1_ready")
        hid2_psum = sem("hid2_psum")
        hid2_ready = sem("hid2_ready")
        y_psum = sem("y_psum")
        y_ready = sem("y_ready")
        y_stored = sem("y_stored")

        def shifted_rows(first, tiles):
            return bass.AP(tensor=scratch, offset=first * COLS,
                           ap=[[ROWS * COLS, CHUNKS], [COLS, FIELDS], [COLS, tiles], [1, COLS]])

        block = ctx.enter_context(nc.Block())

        @block.sync
        def _(sp):
            sp.dma_start(ids_sb[:, :], ids).then_inc(ids_loaded, 16)
            sp.dma_start(base_sb[:, :], field_base).then_inc(ids_loaded, 16)

            def feed(c, s, i, first=False):
                sp.wait_ge(gather_done[s], 16 * PER_GROUP * (i + 1))
                for copy in range(2):
                    for j in range(GROUPS):
                        sp.dma_start(
                            scratch[c, copy * FIELDS:(copy + 1) * FIELDS,
                                    j * PER_GROUP * EMBED:(j + 1) * PER_GROUP * EMBED],
                            gathered[s][j * FIELDS:(j + 1) * FIELDS, :],
                        ).then_inc(scratch_written[s], 16)
                sp.wait_ge(scratch_written[s], 16 * 2 * GROUPS * (i + 1))
                for b in range(BLOCKS):
                    if not first:
                        sp.wait_ge(pair_ready, pair_z2(c - 2, (b + 1) * BLOCK // PAIR - 1) + 1)
                    for q in range(GROUPS):
                        sp.dma_start(
                            xsh[s][q * FIELDS:(q + 1) * FIELDS, b * BLOCK:(b + 1) * BLOCK, :],
                            shifted_rows(SHIFTS[q][b], BLOCK)[c],
                        ).then_inc(xsh_loaded[s][b], 16)
                    if b == 0:
                        for j in range(GROUPS):
                            sp.dma_start(xall[s][j * FIELDS:(j + 1) * FIELDS, :],
                                         scratch[c, 0:FIELDS, :]).then_inc(xall_loaded[s], 16)

            for s in range(2):
                feed(s, s, 0, first=True)
            with sp.Fori(1, CHUNKS // 2) as i:
                for s in range(2):
                    feed(2 * i + s, s, i)
            sp.wait_ge(y_ready, 2)
            sp.dma_start(out.rearrange("b one -> one b"), y_sb[:, :]).then_inc(y_stored, 16)
            sp.wait_ge(y_stored, 16)

        @block.gpsimd
        def _(pool):
            pool.wait_ge(rows_ready, 1)

            def gather(c, s, i, first=False):
                if not first:
                    pool.wait_ge(scratch_written[s], 16 * 2 * GROUPS * i)
                nc.gpsimd.tensor_copy(rows_now[s][:, :], rows_sb[:, bass.ds(c * PER_GROUP, PER_GROUP)]
                                      ).then_inc(rows_staged, 1)
                pool.wait_ge(rows_staged, 1)
                pool.sem_inc(rows_staged, -1)
                for n in range(PER_GROUP):
                    pool.indirect_dma_start(
                        out=gathered[s][:, n * EMBED:(n + 1) * EMBED], out_offset=None,
                        in_=tables,
                        in_offset=bass.IndirectOffsetOnAxis(
                            ap=rows_now[s][:, n:n + 1], axis=0),
                    ).then_inc(gather_done[s], 16)

            for s in range(2):
                gather(s, s, 0, first=True)
            with pool.Fori(1, CHUNKS // 2) as i:
                for s in range(2):
                    gather(2 * i + s, s, i)

        @block.scalar
        def _(act):
            act.dma_start(w0a_sb[:, :, :], w0a).then_inc(w0_loaded, 16)
            act.dma_start(w0b_sb[:, :, :], w0b).then_inc(w0_loaded, 16)
            act.dma_start(w0ma_sb[MIDQ:MIDQ + MIDN, :], w0ma).then_inc(w0_loaded, 16)
            act.dma_start(w0mb_sb[MIDQ:MIDQ + MIDN, :], w0mb).then_inc(w0_loaded, 16)
            for n, b in enumerate((bias0, bias1, bias2)):
                act.dma_start(bias[n][:, :], b).then_inc(bias_loaded, 16)
            act.dma_start(w1_sb[:, :, :], w1).then_inc(w1_loaded, 16)
            act.dma_start(w2_sb[:, :, :], w2).then_inc(w2_loaded, 16)
            top = [(wt1_sb[:, :, :], wt1[0:2 * 128, :].rearrange("(t p) n -> p t n", p=128)),
                   (wt1d_sb[:, :], wt1[2 * 128:2 * 128 + DENSE, :]),
                   (dense_sb[:, :], dense_t), (bt1_sb[:, :], bt1),
                   (wt2_sb[:, :, :], wt2.rearrange("(t p) n -> p t n", p=128)),
                   (bt2_sb[:, :], bt2), (wt3_sb[:, :], wt3)]
            for dst, src in top:
                act.dma_start(dst, src).then_inc(top_loaded, 16)
            act.wait_ge(bias_loaded, 3 * 16)

            def relu(dst, src, b):
                return nc.scalar.activation(dst, src, ACT.Relu, bias=b)

            def after_layer0(c, s):
                act.wait_ge(y0_ready, c + 1)
                if not (isinstance(c, int) and c == 0):
                    act.wait_ge(pair_ready, pair_z1(c - 1, L12_PAIRS - 1) + 1)
                relu(h1[0:HALF, :], y0[s][HALF:MAPS, :], bias[0][HALF:MAPS, :])
                relu(h1[HALF:MAPS, :], y0[s][HALF:MAPS, :], bias[0][HALF:MAPS, :]).then_inc(h1_ready, 1)
                if not (isinstance(c, int) and c < 2):
                    act.wait_ge(pooled01, c - 1)
                relu(kept01[s][0:HALF, :], y0[s][0:HALF, :], bias[0][0:HALF, :]).then_inc(kept0_ready, 1)

            def chunk(c, s, i, first=False, last=False):
                act.wait_ge(pair_used, pair_z1(c, L12_PAIRS - 1) + 1)
                relu(h2[0:HALF, :], y1[s][0:HALF, :], bias[1][0:HALF, :])
                relu(h2[HALF:MAPS, :], y1[s][0:HALF, :], bias[1][0:HALF, :]).then_inc(h2_ready, 1)
                relu(kept01[s][HALF:MAPS, :], y1[s][HALF:MAPS, :], bias[1][HALF:MAPS, :]).then_inc(kept1_ready, 1)
                if not last:
                    after_layer0(c + 1, 1 - s)
                act.wait_ge(pair_used, pair_z2(c, L12_PAIRS - 1) + 1)
                if not first:
                    act.wait_ge(pooled2, c - 1)
                relu(kept2[s][:, :], y2[s][:, :], bias[2][:, :]).then_inc(kept2_ready, 1)

            after_layer0(0, 0)
            for s in range(2):
                chunk(s, s, 0, first=True)
            with act.Fori(1, CHUNKS // 2 - 1) as i:
                for s in range(2):
                    chunk(2 * i + s, s, i)
            for s in range(2):
                chunk(CHUNKS - 2 + s, s, CHUNKS // 2 - 1, last=s == 1)

            act.wait_ge(top_loaded, TOP_LOADS * 16)
            for n in range(2):
                for m in range(HID1 // 128):
                    act.wait_ge(hid1_psum, n * (HID1 // 128) + m + 1)
                    relu(hid1[:, m, n * COLS:(n + 1) * COLS], banks[n * 4 + m][:, :],
                         bt1_sb[:, m:m + 1]).then_inc(hid1_ready, 1)
            for n in range(2):
                for m in range(HID2 // 128):
                    act.wait_ge(hid2_psum, n * (HID2 // 128) + m + 1)
                    relu(hid2[:, m, n * COLS:(n + 1) * COLS], banks[n * 2 + m][:, :],
                         bt2_sb[:, m:m + 1]).then_inc(hid2_ready, 1)
            for n in range(2):
                act.wait_ge(y_psum, n + 1)
                nc.scalar.copy(y_sb[0:1, n * COLS:(n + 1) * COLS], banks[4 + n][0:1, :]).then_inc(y_ready, 1)

        @block.vector
        def _(dve):
            dve.wait_ge(ids_loaded, 2 * 16)
            nc.vector.tensor_scalar(rows_sb[:, :], ids_sb[:, :], base_sb[:, 0:1], None,
                                    ALU.add).then_inc(rows_ready, 1)
            dve.wait_ge(w0_loaded, 4 * 16)
            nc.vector.tensor_copy(w0[0:FIELDS, 0, :], w0a_sb[0:FIELDS, 0, :]).then_inc(w0_ready, 1)
            for q in range(1, GROUPS):
                part = slice(q * FIELDS, (q + 1) * FIELDS)
                nc.vector.tensor_tensor(w0[part, 0, :], w0a_sb[part, 0, :], w0b_sb[part, 0, :],
                                        ALU.add).then_inc(w0_ready, 1)
            nc.vector.tensor_tensor(w0[:, 1:BLOCK, :], w0a_sb[:, 1:BLOCK, :], w0b_sb[:, 1:BLOCK, :],
                                    ALU.add).then_inc(w0_ready, 1)
            mid = slice(MIDQ, MIDQ + MIDN)
            nc.vector.tensor_tensor(w0m[mid, :], w0ma_sb[mid, :], w0mb_sb[mid, :],
                                    ALU.add).then_inc(w0_ready, 1)

            def product_pair(n, slot, xs, pair, other):
                if not (isinstance(n, int) and n < ZRING):
                    dve.wait_ge(pair_used, n - ZRING + 1)
                nc.vector.tensor_tensor(z[slot][:, :, :], xs[:, pair * PAIR:(pair + 1) * PAIR, :],
                                        other, ALU.mult).then_inc(pair_ready, 1)

            def twice(t):
                return t[:, :].unsqueeze(1).to_broadcast([128, PAIR, COLS])

            def layer0(c, s, i):
                dve.wait_ge(xall_loaded[s], 16 * GROUPS * (i + 1))
                dve.wait_ge(xsh_loaded[s][0], 16 * GROUPS * (i + 1))
                for g in range(L0_PAIRS):
                    n = pair_z0(c, g)
                    product_pair(n, slot_z0(c, s, g), xsh[s], g, twice(xall[s]))
                dve.wait_ge(xsh_loaded[s][MID // BLOCK], 16 * GROUPS * (i + 1))
                if not (isinstance(c, int) and c == 0):
                    dve.wait_ge(y0_ready, c)
                nc.vector.tensor_tensor(zmid[mid, :], xsh[s][mid, MID, :], xall[s][mid, :],
                                        ALU.mult).then_inc(mid_ready, 1)

            def pool_kept2(c, s):
                dve.wait_ge(kept2_ready, c + 1)
                nc.vector.tensor_reduce(pool2[:, bass.ds(c * SAMPLES, SAMPLES)],
                                        kept2[s][:, :].rearrange("p (b e) -> p b e", e=EMBED),
                                        axis=AX.X, op=ALU.add).then_inc(pooled2, 1)

            def pool_kept01(c, s):
                dve.wait_ge(kept0_ready, c + 1)
                dve.wait_ge(kept1_ready, c + 1)
                nc.vector.tensor_reduce(pool01[:, bass.ds(c * SAMPLES, SAMPLES)],
                                        kept01[s][:, :].rearrange("p (b e) -> p b e", e=EMBED),
                                        axis=AX.X, op=ALU.add).then_inc(pooled01, 1)

            def chunk(c, s, i, first=False, last=False):
                dve.wait_ge(h1_ready, c + 1)
                for g in range(L12_PAIRS):
                    if g % (BLOCK // PAIR) == 0:
                        dve.wait_ge(xsh_loaded[s][g * PAIR // BLOCK], 16 * GROUPS * (i + 1))
                    product_pair(pair_z1(c, g), slot_z1(s, g), xsh[s], g, twice(h1))
                    if g == 2 and not first:
                        pool_kept2(c - 1, 1 - s)
                if not last:
                    layer0(c + 1, 1 - s, i + s)
                dve.wait_ge(h2_ready, c + 1)
                for g in range(L12_PAIRS):
                    product_pair(pair_z2(c, g), slot_z2(s, g, last), xsh[s], g, twice(h2))
                    if g == 2:
                        pool_kept01(c, s)

            layer0(0, 0, 0)
            for s in range(2):
                chunk(s, s, 0, first=s == 0)
            with dve.Fori(1, CHUNKS // 2 - 1) as i:
                for s in range(2):
                    chunk(2 * i + s, s, i)
            for s in range(2):
                chunk(CHUNKS - 2 + s, s, CHUNKS // 2 - 1, last=s == 1)
            pool_kept2(CHUNKS - 1, 1)

        @block.tensor
        def _(pe):
            def contract(bank, pairs, weights, number, slot, close=True):
                for g in range(pairs):
                    pe.wait_ge(pair_ready, number(g) + 1)
                    for t in range(PAIR):
                        last = nc.tensor.matmul(bank[:, :], weights[:, g * PAIR + t, :],
                                                z[slot(g)][:, t, :],
                                                start=g == 0 and t == 0,
                                                stop=close and g == pairs - 1 and t == PAIR - 1)
                    last.then_inc(pair_used, 1)

            def layer0(c, s):
                if not (isinstance(c, int) and c < 2):
                    pe.wait_ge(kept0_ready, c - 1)
                contract(y0[s], L0_PAIRS, w0, lambda g: pair_z0(c, g), lambda g: slot_z0(c, s, g),
                         close=False)
                pe.wait_ge(mid_ready, c + 1)
                nc.tensor.matmul(y0[s][:, :], w0m[MIDQ:MIDQ + MIDN, :], zmid[MIDQ:MIDQ + MIDN, :],
                                 start=False, stop=True).then_inc(y0_ready, 1)

            def chunk(c, s, first=False, last=False):
                if not first:
                    pe.wait_ge(kept1_ready, c - 1)
                contract(y1[s], L12_PAIRS, w1_sb, lambda g: pair_z1(c, g), lambda g: slot_z1(s, g))
                if not last:
                    layer0(c + 1, 1 - s)
                if not first:
                    pe.wait_ge(kept2_ready, c - 1)
                contract(y2[s], L12_PAIRS, w2_sb, lambda g: pair_z2(c, g),
                         lambda g: slot_z2(s, g, last))

            pe.wait_ge(w0_ready, GROUPS + 2)
            layer0(0, 0)
            pe.wait_ge(w1_loaded, 16)
            pe.wait_ge(w2_loaded, 16)
            for s in range(2):
                chunk(s, s, first=True)
            with pe.Fori(1, CHUNKS // 2 - 1) as i:
                for s in range(2):
                    chunk(2 * i + s, s)
            for s in range(2):
                chunk(CHUNKS - 2 + s, s, last=s == 1)

            pe.wait_ge(top_loaded, TOP_LOADS * 16)
            pe.wait_ge(pooled01, CHUNKS)
            pe.wait_ge(pooled2, CHUNKS)
            for n in range(2):
                cols = slice(n * COLS, (n + 1) * COLS)
                for m in range(HID1 // 128):
                    maps = slice(m * 128, (m + 1) * 128)
                    bank = banks[n * 4 + m]
                    nc.tensor.matmul(bank[:, :], wt1_sb[:, 0, maps], pool01[:, cols], start=True, stop=False)
                    nc.tensor.matmul(bank[:, :], wt1_sb[:, 1, maps], pool2[:, cols], start=False, stop=False)
                    nc.tensor.matmul(bank[:, :], wt1d_sb[:, maps], dense_sb[:, cols],
                                     start=False, stop=True).then_inc(hid1_psum, 1)
            for n in range(2):
                cols = slice(n * COLS, (n + 1) * COLS)
                pe.wait_ge(hid1_ready, (n + 1) * (HID1 // 128))
                for m in range(HID2 // 128):
                    for k in range(HID1 // 128):
                        last = nc.tensor.matmul(banks[n * 2 + m][:, :],
                                                wt2_sb[:, k, m * 128:(m + 1) * 128], hid1[:, k, cols],
                                                start=k == 0, stop=k == HID1 // 128 - 1)
                    last.then_inc(hid2_psum, 1)
            for n in range(2):
                cols = slice(n * COLS, (n + 1) * COLS)
                pe.wait_ge(hid2_ready, (n + 1) * (HID2 // 128))
                for k in range(HID2 // 128):
                    last = nc.tensor.matmul(banks[4 + n][0:1, :], wt3_sb[:, k:k + 1], hid2[:, k, cols],
                                            start=k == 0, stop=k == HID2 // 128 - 1)
                last.then_inc(y_psum, 1)


def kernel(**inputs):
    import numpy as np
    import concourse.bacc as bacc
    from concourse.bass_utils import run_bass_kernel_spmd

    a = {k: np.asarray(v) for k, v in inputs.items()}
    tables = [a[f"tbl_{f}"] for f in range(FIELDS)]
    first_row = np.cumsum([0] + [t.shape[0] for t in tables[:-1]])
    ids = a["ids"].reshape(CHUNKS, GROUPS, PER_GROUP, FIELDS).transpose(1, 3, 0, 2)

    p = np.arange(128)[:, None]
    shifts = np.array([[shift(k, q) for k in range(TILES)] for q in range(GROUPS)])[p[:, 0] // FIELDS]
    field = (p % FIELDS + shifts) % FIELDS
    w0 = a["L0_rec_W0"].reshape(MAPS, FIELDS, FIELDS)
    own, other = np.broadcast_to(p % FIELDS, (128, BLOCK)), field[:, :BLOCK]
    mid = np.arange(MIDN)
    w1 = a["L0_rec_W1"].reshape(MAPS, FIELDS, HALF)
    w2 = a["L0_rec_W2"].reshape(MAPS, FIELDS, HALF)
    swap = np.r_[HALF:MAPS, 0:HALF]
    arrays = {
        "tables": np.concatenate(tables, axis=0),
        "ids": ids.reshape(128, CHUNKS * PER_GROUP),
        "field_base": np.tile(first_row, GROUPS).astype(np.float32)[:, None],
        "dense_t": a["dense_ctx"].T,
        "w0a": w0[:, own, other].transpose(1, 2, 0),
        "w0b": w0[:, other, own].transpose(1, 2, 0),
        "w0ma": w0[:, mid, mid + MIDN].T,
        "w0mb": w0[:, mid + MIDN, mid].T,
        "w1": w1[swap][:, field, p % HALF].transpose(1, 2, 0),
        "w2": w2[:, field, p % HALF].transpose(1, 2, 0),
        "bias0": a["L0_rec_b0"][:, None],
        "bias1": a["L0_rec_b1"][swap][:, None],
        "bias2": a["L0_rec_b2"][:, None],
        "wt1": a["W_top1"],
        "bt1": a["b_top1"].reshape(HID1 // 128, 128).T,
        "wt2": a["W_top2"],
        "bt2": a["b_top2"].reshape(HID2 // 128, 128).T,
        "wt3": a["W_top3"].reshape(HID2 // 128, 128).T,
    }
    nc = bacc.Bacc("TRN2", target_bir_lowering=False, num_devices=1)
    arrays = {f"in_{k}": np.ascontiguousarray(v) for k, v in arrays.items()}
    args = [nc.dram_tensor(k, v.shape, mybir.dt.from_np(v.dtype), kind="ExternalInput").ap()
            for k, v in arrays.items()]
    args.append(nc.dram_tensor("out_y", (BATCH, 1), mybir.dt.float32, kind="ExternalOutput").ap())
    dlrm_tower(nc, *args)
    return run_bass_kernel_spmd(nc, [arrays], core_ids=[0]).results[0]["out_y"]
```

```python
import concourse.bass as bass
from concourse import mybir
from contextlib import ExitStack

FIELDS = 32
EMBED = 16
BATCH = 1024
MAPS = 128
HALF = MAPS // 2
GROUPS = 4
SAMPLES = 32
CHUNKS = BATCH // SAMPLES
COLS = SAMPLES * EMBED
PER_GROUP = SAMPLES // GROUPS
TILES = FIELDS * HALF // 128
BLOCK = 4
BLOCKS = TILES // BLOCK
PAIR = 2
PAIRS = TILES // PAIR
SHIFTS = [[0, 8, 12, 16], [8, 16, 20, 24], [4, 20, 24, 28], [12, 28, 0, 4]]
MID = BLOCK
MIDN = FIELDS // 2
MID_HH, MID_LH, MID_HL = (slice(q * FIELDS, q * FIELDS + MIDN) for q in (1, 2, 3))
ROWS = 2 * FIELDS
DENSE = 16
HID1, HID2 = 512, 256
TOP_LOADS = 7

KIND = ["P", "W", "D", "P", "W", "D", "P", "W"]
ORDER = {k: [g for g in range(PAIRS) if KIND[g] == k] for k in "WPD"}
MAKE = [0, 1, 2, 3, 4, ("low", 2), 5, 6, 7, ("low", 5)]
USE = [1, 0, 4, 2, 3, 7, 5, 6]
SPLIT = [g for g in range(PAIRS) if KIND[g] != "W"]
L0_PAIRS = 2
NW, NP, ND = (len(ORDER[k]) for k in "WPD")
WRING, PRING, DRING = 4, 3, 2
W_CHUNK = 2 * NW + L0_PAIRS
assert W_CHUNK % WRING == 0 and 2 * NP % PRING == 0 and 2 * ND % DRING == 0


def shift(k, quarter):
    return SHIFTS[quarter][k // BLOCK] + k % BLOCK


def is_last(c):
    return isinstance(c, int) and c == CHUNKS - 1


def whole0(c, g):
    return g if isinstance(c, int) and c == 0 else L0_PAIRS + W_CHUNK * (c - 1) + NW + g


def number(layer, c, g):
    kind, j = KIND[g], ORDER[KIND[g]].index(g)
    if kind == "W":
        before = 0 if layer == 1 else NW + (0 if is_last(c) else L0_PAIRS)
        return L0_PAIRS + W_CHUNK * c + before + j
    n = NP if kind == "P" else ND
    return 2 * n * c + (layer - 1) * n + j


def slot0(c, g):
    return (g if isinstance(c, int) and c == 0 else L0_PAIRS + NW + g) % WRING


def slot(layer, c, g):
    kind = KIND[g]
    at_zero = number(layer, CHUNKS - 1 if is_last(c) else 0, g)
    return at_zero % {"W": WRING, "P": PRING, "D": DRING}[kind]


def wait(eng, semaphore, count):
    if not (isinstance(count, int) and count < 1):
        eng.wait_ge(semaphore, count)


def dlrm_tower(nc, tables, ids, field_base, dense_t, w0a, w0b, w0ma, w0mb,
               w1_whole, w1_split, w2_whole, w2_split,
               bias0, bias1, bias2, wt1, bt1, wt2, bt2, wt3, out):
    fp32 = mybir.dt.float32
    fp32r = mybir.dt.float32r
    i32 = mybir.dt.int32
    ALU = mybir.AluOpType
    ACT = mybir.ActivationFunctionType
    AX = mybir.AxisListType

    ctx = ExitStack()
    with ctx:
        def sb(name, shape, dt=fp32):
            return ctx.enter_context(nc.sbuf_tensor(name, shape, dt))

        def sem(name):
            return ctx.enter_context(nc.semaphore(name))

        scratch = nc.dram_tensor("x_scratch", [CHUNKS, ROWS, COLS], fp32, kind="Internal")

        ids_sb = sb("ids_sb", [128, CHUNKS * PER_GROUP], i32)
        base_sb = sb("base_sb", [128, 1])
        rows_sb = sb("rows_sb", [128, CHUNKS * PER_GROUP], i32)
        rows_now = [sb(f"rows_now{s}", [128, PER_GROUP], i32) for s in range(2)]
        gathered = [sb(f"gathered{s}", [128, PER_GROUP * EMBED]) for s in range(2)]
        xsh = [sb(f"xsh{s}", [128, TILES, COLS]) for s in range(2)]
        xall = [sb(f"xall{s}", [128, COLS]) for s in range(2)]
        whole = [sb(f"whole{s}", [128, PAIR, COLS]) for s in range(WRING)]
        pfull = sb("pfull", [128, PRING, PAIR, COLS])
        phigh = [sb(f"phigh{s}", [128, PAIR, COLS], fp32r) for s in range(PRING)]
        plow = [sb(f"plow{s}", [128, PAIR, COLS], fp32r) for s in range(PRING)]
        dhigh = [sb(f"dhigh{s}", [128, PAIR, COLS], fp32r) for s in range(DRING)]
        dlow = [sb(f"dlow{s}", [128, PAIR, COLS], fp32r) for s in range(DRING)]
        midfull = sb("midfull", [128, COLS])
        midhigh = sb("midhigh", [128, COLS], fp32r)
        zmid = sb("zmid", [128, COLS], fp32r)
        kept01 = [sb(f"kept01{s}", [128, COLS]) for s in range(2)]
        kept2 = [sb(f"kept2{s}", [128, COLS]) for s in range(2)]
        pool01 = sb("pool01", [128, BATCH])
        pool2 = sb("pool2", [128, BATCH])
        w0ma_sb = sb("w0ma_sb", [128, MAPS])
        w0mb_sb = sb("w0mb_sb", [128, MAPS])
        w0 = sb("w0", [128, BLOCK, MAPS])
        w0m = sb("w0m", [128, MAPS])
        wmid = sb("wmid", [128, MAPS], fp32r)
        ww = {n: sb(f"w{n}_whole", [128, PAIR * NW, MAPS]) for n in (1, 2)}
        wh = {n: sb(f"w{n}_high", [128, PAIR * len(SPLIT), MAPS], fp32r) for n in (1, 2)}
        wl = {n: sb(f"w{n}_low", [128, PAIR * len(SPLIT), MAPS], fp32r) for n in (1, 2)}
        bias = [sb(f"bias{n}_sb", [128, 1]) for n in range(3)]
        wt1_sb = sb("wt1_sb", [128, 2, HID1])
        wt1d_sb = sb("wt1d_sb", [DENSE, HID1])
        dense_sb = sb("dense_sb", [DENSE, BATCH])
        bt1_sb = sb("bt1_sb", [128, HID1 // 128])
        wt2_sb = sb("wt2_sb", [128, HID1 // 128, HID2])
        bt2_sb = sb("bt2_sb", [128, HID2 // 128])
        wt3_sb = sb("wt3_sb", [128, HID2 // 128])
        hid1 = xsh[0][:, 0:HID1 // 128 * 2, :].rearrange("p (m h) n -> p m (h n)", h=2)
        hid2 = xsh[1][:, 0:HID2 // 128 * 2, :].rearrange("p (m h) n -> p m (h n)", h=2)
        flat = pfull[:, :, :, :].rearrange("p s t n -> p (s t n)")
        n_split = PAIR * len(SPLIT) * MAPS
        wraw = {n: flat[:, (n - 1) * n_split:n * n_split].rearrange("p (t m) -> p t m", m=MAPS)
                for n in (1, 2)}
        w0a_sb = whole[2][:, 0, :].rearrange("p (t m) -> p t m", m=MAPS)
        w0b_sb = whole[2][:, 1, :].rearrange("p (t m) -> p t m", m=MAPS)
        y_sb = whole[3][0:1, :, :].rearrange("p t n -> p (t n)")

        banks = ctx.enter_context(nc.psum_tensor("banks", [128, 8, COLS], fp32))
        y0, y1, y2 = (banks[:, n, :] for n in range(3))
        h1, h2 = (banks[:, n, :] for n in range(3, 5))
        xps = banks[:, 5, :]
        dfull = banks[:, 6:8, :]

        ids_loaded = sem("ids_loaded")
        rows_ready = sem("rows_ready")
        rows_staged = sem("rows_staged")
        gather_done = [sem(f"gather_done{s}") for s in range(2)]
        scratch_written = [sem(f"scratch_written{s}") for s in range(2)]
        xall_loaded = [sem(f"xall_loaded{s}") for s in range(2)]
        xsh_loaded = [[sem(f"xsh_loaded{s}_{b}") for b in range(BLOCKS)] for s in range(2)]
        w0_loaded = sem("w0_loaded")
        w12_loaded = sem("w12_loaded")
        bias_loaded = sem("bias_loaded")
        top_loaded = sem("top_loaded")
        w0_ready = sem("w0_ready")
        weights_staged = sem("weights_staged")
        high_weights = sem("high_weights")
        low_weights = sem("low_weights")
        xps_ready = sem("xps_ready")
        made = {k: sem(f"made_{k}") for k in "WPD"}
        high = {k: sem(f"high_{k}") for k in "PD"}
        low = {k: sem(f"low_{k}") for k in "PD"}
        used = {k: sem(f"used_{k}") for k in "WPD"}
        zeroed = sem("zeroed")
        mid_full = sem("mid_full")
        mid_rounded = sem("mid_rounded")
        mid_high = sem("mid_high")
        mid_low = sem("mid_low")
        y0_ready = sem("y0_ready")
        h1_ready = sem("h1_ready")
        h2_ready = sem("h2_ready")
        kept0_ready = sem("kept0_ready")
        kept1_ready = sem("kept1_ready")
        kept2_ready = sem("kept2_ready")
        pooled01 = sem("pooled01")
        pooled2 = sem("pooled2")
        hid1_psum = sem("hid1_psum")
        hid1_ready = sem("hid1_ready")
        hid2_psum = sem("hid2_psum")
        hid2_ready = sem("hid2_ready")
        y_psum = sem("y_psum")
        y_ready = sem("y_ready")
        y_stored = sem("y_stored")

        def shifted_rows(first, tiles):
            return bass.AP(tensor=scratch, offset=first * COLS,
                           ap=[[ROWS * COLS, CHUNKS], [COLS, FIELDS], [COLS, tiles], [1, COLS]])

        block = ctx.enter_context(nc.Block())

        def both_copies(j):
            return bass.AP(tensor=scratch, offset=j * PER_GROUP * EMBED,
                           ap=[[ROWS * COLS, CHUNKS], [COLS, FIELDS], [FIELDS * COLS, 2],
                               [1, PER_GROUP * EMBED]])

        def out_ready(eng, layer, c):
            g = USE[-1]
            eng.wait_ge(used[KIND[g]], number(layer, c, g) + 1)

        @block.sync
        def _(sp):
            sp.dma_start(ids_sb[:, :], ids).then_inc(ids_loaded, 16)
            sp.dma_start(base_sb[:, :], field_base).then_inc(ids_loaded, 16)

            def feed(c, s, i, first=False):
                sp.wait_ge(gather_done[s], 16 * PER_GROUP * (i + 1))
                for j in range(GROUPS):
                    sp.dma_start(
                        both_copies(j)[c],
                        gathered[s][j * FIELDS:(j + 1) * FIELDS, :].unsqueeze(1)
                        .to_broadcast([FIELDS, 2, PER_GROUP * EMBED]),
                    ).then_inc(scratch_written[s], 16)
                sp.wait_ge(scratch_written[s], 16 * GROUPS * (i + 1))
                for b in range(BLOCKS):
                    if not first:
                        g = b * BLOCK // PAIR + 1
                        sp.wait_ge(made[KIND[g]], number(2, c - 2, g) + 1)
                    for q in range(GROUPS):
                        sp.dma_start(
                            xsh[s][q * FIELDS:(q + 1) * FIELDS, b * BLOCK:(b + 1) * BLOCK, :],
                            shifted_rows(SHIFTS[q][b], BLOCK)[c],
                        ).then_inc(xsh_loaded[s][b], 16)
                    if b == 0:
                        for j in range(GROUPS):
                            sp.dma_start(xall[s][j * FIELDS:(j + 1) * FIELDS, :],
                                         scratch[c, 0:FIELDS, :]).then_inc(xall_loaded[s], 16)

            for s in range(2):
                feed(s, s, 0, first=True)
            with sp.Fori(1, CHUNKS // 2) as i:
                for s in range(2):
                    feed(2 * i + s, s, i)
            sp.wait_ge(y_ready, 2)
            sp.dma_start(out.rearrange("b one -> one b"), y_sb).then_inc(y_stored, 16)
            sp.wait_ge(y_stored, 16)

        @block.gpsimd
        def _(pool):
            def stage_rows(c, s):
                nc.gpsimd.tensor_copy(rows_now[s][:, :], rows_sb[:, bass.ds(c * PER_GROUP, PER_GROUP)]
                                      ).then_inc(rows_staged, 1)
                pool.wait_ge(rows_staged, 1)
                pool.sem_inc(rows_staged, -1)

            def gather(s, n):
                pool.indirect_dma_start(
                    out=gathered[s][:, n * EMBED:(n + 1) * EMBED], out_offset=None,
                    in_=tables,
                    in_offset=bass.IndirectOffsetOnAxis(ap=rows_now[s][:, n:n + 1], axis=0),
                ).then_inc(gather_done[s], 16)

            def take_low(layer, c, g):
                n, k = number(layer, c, g), slot(layer, c, g)
                pool.wait_ge(high["P"], n + 1)
                wait(pool, used["P"], n - PRING + 1)
                nc.gpsimd.tensor_tensor(plow[k][:, :, :], pfull[:, k, :, :], phigh[k][:, :, :],
                                        ALU.subtract).then_inc(low["P"], 1)

            def take_mid_low(c):
                pool.wait_ge(mid_high, c + 1)
                wait(pool, y0_ready, c)
                nc.gpsimd.tensor_tensor(zmid[:, :], midfull[:, :], midhigh[:, :],
                                        ALU.subtract).then_inc(mid_low, 1)

            half = PER_GROUP // 2
            share = [half // NP] * NP
            share[0] += half % NP

            def free_buffer(s, i):
                pool.wait_ge(scratch_written[s], 16 * GROUPS * (i + 1))

            def chunk(c, s, i):
                for layer, ahead, first in ((1, 2, half), (2, 3, 0)):
                    gathers = not (isinstance(c, int) and c + ahead >= CHUNKS)
                    to = s if ahead == 2 else 1 - s
                    if gathers and first == 0:
                        free_buffer(to, i + s)
                        stage_rows(c + ahead, to)
                    n = first
                    for j, g in enumerate(ORDER["P"]):
                        take_low(layer, c, g)
                        if layer == 1 and j == NP - 1 and not is_last(c):
                            take_mid_low(c + 1)
                        for _ in range(share[j] if gathers else 0):
                            gather(to, n)
                            n += 1

            pool.wait_ge(rows_ready, 1)
            for s in range(2):
                stage_rows(s, s)
                for n in range(PER_GROUP):
                    gather(s, n)
            free_buffer(0, 0)
            stage_rows(2, 0)
            for n in range(half):
                gather(0, n)
            take_mid_low(0)
            for s in range(2):
                chunk(s, s, 0)
            with pool.Fori(1, CHUNKS // 2 - 2) as i:
                for s in range(2):
                    chunk(2 * i + s, s, i)
            for c in range(CHUNKS - 4, CHUNKS):
                chunk(c, c % 2, c // 2)

        @block.scalar
        def _(act):
            act.dma_start(w0a_sb, w0a).then_inc(w0_loaded, 16)
            act.dma_start(w0b_sb, w0b).then_inc(w0_loaded, 16)
            act.dma_start(w0ma_sb[MID_HH, :], w0ma).then_inc(w0_loaded, 16)
            act.dma_start(w0mb_sb[MID_HH, :], w0mb).then_inc(w0_loaded, 16)
            for n, b in enumerate((bias0, bias1, bias2)):
                act.dma_start(bias[n][:, :], b).then_inc(bias_loaded, 16)
            for n, w in ((1, w1_split), (2, w2_split)):
                act.dma_start(wraw[n], w).then_inc(weights_staged, 16)
            for n, w in ((1, w1_whole), (2, w2_whole)):
                act.dma_start(ww[n][:, :, :], w).then_inc(w12_loaded, 16)
            act.wait_ge(w0_ready, GROUPS + 2)
            act.wait_ge(zeroed, 3)
            nc.scalar.copy(wmid[MID_HH, :], w0m[MID_HH, :])
            nc.scalar.copy(wmid[MID_HL, :], w0m[MID_HH, :]).then_inc(high_weights, 1)
            act.wait_ge(weights_staged, 2 * 16)
            for n in (1, 2):
                nc.scalar.copy(wh[n][:, :, :], wraw[n]).then_inc(high_weights, 1)
            top = [(wt1_sb[:, :, :], wt1[0:2 * 128, :].rearrange("(t p) n -> p t n", p=128)),
                   (wt1d_sb[:, :], wt1[2 * 128:2 * 128 + DENSE, :]),
                   (dense_sb[:, :], dense_t), (bt1_sb[:, :], bt1),
                   (wt2_sb[:, :, :], wt2.rearrange("(t p) n -> p t n", p=128)),
                   (bt2_sb[:, :], bt2), (wt3_sb[:, :], wt3)]
            act.wait_ge(bias_loaded, 3 * 16)

            def relu(dst, src, b):
                return nc.scalar.activation(dst, src, ACT.Relu, bias=b)

            def copy_x(c, s, i):
                act.wait_ge(xall_loaded[s], 16 * GROUPS * (i + 1))
                if not (isinstance(c, int) and c == 0):
                    act.wait_ge(made["W"], whole0(c - 1, L0_PAIRS - 1) + 1)
                nc.scalar.copy(xps, xall[s][:, :]).then_inc(xps_ready, 1)

            def take_high(layer, c, g):
                kind, n, k = KIND[g], number(layer, c, g), slot(layer, c, g)
                full = pfull[:, k, :, :] if kind == "P" else dfull
                act.wait_ge(made[kind], n + 1)
                wait(act, used[kind], n - (PRING if kind == "P" else DRING) + 1)
                nc.scalar.copy((phigh if kind == "P" else dhigh)[k][:, :, :], full
                               ).then_inc(high[kind], 1)

            def take_mid_high(c):
                act.wait_ge(mid_full, c + 1)
                nc.scalar.copy(midhigh[MID_HL, :], midfull[MID_HL, :]).then_inc(mid_rounded, 1)
                act.wait_ge(mid_rounded, c + 1)
                nc.scalar.copy(midfull[MID_LH, :], midhigh[MID_HL, :])
                nc.scalar.copy(midfull[MID_HH, :], midhigh[MID_HL, :]).then_inc(mid_high, 1)

            def after_layer0(c, s):
                act.wait_ge(y0_ready, c + 1)
                if not (isinstance(c, int) and c == 0):
                    g = PAIRS - 1
                    act.wait_ge(made[KIND[g]], number(1, c - 1, g) + 1)
                relu(h1[0:HALF, :], y0[HALF:MAPS, :], bias[0][HALF:MAPS, :])
                relu(h1[HALF:MAPS, :], y0[HALF:MAPS, :], bias[0][HALF:MAPS, :]).then_inc(h1_ready, 1)
                wait(act, pooled01, c - 1)
                relu(kept01[s][0:HALF, :], y0[0:HALF, :], bias[0][0:HALF, :]).then_inc(kept0_ready, 1)

            def after_layer2(c, s):
                out_ready(act, 2, c)
                wait(act, pooled2, c - 1)
                relu(kept2[s][:, :], y2, bias[2][:, :]).then_inc(kept2_ready, 1)

            def chunk(c, s, i, first=False, last=False):
                take_high(1, c, SPLIT[0])
                if not last:
                    copy_x(c + 1, 1 - s, i + s)
                for g in SPLIT[1:3]:
                    take_high(1, c, g)
                if not first:
                    after_layer2(c - 1, 1 - s)
                take_high(1, c, SPLIT[3])
                take_high(1, c, SPLIT[4])
                if not last:
                    take_mid_high(c + 1)
                out_ready(act, 1, c)
                relu(h2[0:HALF, :], y1[0:HALF, :], bias[1][0:HALF, :])
                relu(h2[HALF:MAPS, :], y1[0:HALF, :], bias[1][0:HALF, :]).then_inc(h2_ready, 1)
                take_high(2, c, SPLIT[0])
                relu(kept01[s][HALF:MAPS, :], y1[HALF:MAPS, :], bias[1][HALF:MAPS, :]
                     ).then_inc(kept1_ready, 1)
                for g in SPLIT[1:3]:
                    take_high(2, c, g)
                if not last:
                    after_layer0(c + 1, 1 - s)
                for g in SPLIT[3:]:
                    take_high(2, c, g)

            copy_x(0, 0, 0)
            take_mid_high(0)
            after_layer0(0, 0)
            for s in range(2):
                chunk(s, s, 0, first=s == 0)
            for dst, src in top:
                act.dma_start(dst, src).then_inc(top_loaded, 16)
            with act.Fori(1, CHUNKS // 2 - 1) as i:
                for s in range(2):
                    chunk(2 * i + s, s, i)
            for s in range(2):
                chunk(CHUNKS - 2 + s, s, CHUNKS // 2 - 1, last=s == 1)
            after_layer2(CHUNKS - 1, 1)

            act.wait_ge(top_loaded, TOP_LOADS * 16)
            for n in range(2):
                for m in range(HID1 // 128):
                    act.wait_ge(hid1_psum, n * (HID1 // 128) + m + 1)
                    relu(hid1[:, m, n * COLS:(n + 1) * COLS], banks[:, n * 4 + m, :],
                         bt1_sb[:, m:m + 1]).then_inc(hid1_ready, 1)
            for n in range(2):
                for m in range(HID2 // 128):
                    act.wait_ge(hid2_psum, n * (HID2 // 128) + m + 1)
                    relu(hid2[:, m, n * COLS:(n + 1) * COLS], banks[:, n * 2 + m, :],
                         bt2_sb[:, m:m + 1]).then_inc(hid2_ready, 1)
            for n in range(2):
                act.wait_ge(y_psum, n + 1)
                nc.scalar.copy(y_sb[:, n * COLS:(n + 1) * COLS], banks[0:1, 4 + n, :]).then_inc(y_ready, 1)

        @block.vector
        def _(dve):
            dve.wait_ge(ids_loaded, 2 * 16)
            nc.vector.tensor_scalar(rows_sb[:, :], ids_sb[:, :], base_sb[:, 0:1], None,
                                    ALU.add).then_inc(rows_ready, 1)
            dve.wait_ge(w0_loaded, 4 * 16)
            nc.vector.tensor_copy(w0[0:FIELDS, 0, :], w0a_sb[0:FIELDS, 0, :]).then_inc(w0_ready, 1)
            for q in range(1, GROUPS):
                part = slice(q * FIELDS, (q + 1) * FIELDS)
                nc.vector.tensor_tensor(w0[part, 0, :], w0a_sb[part, 0, :], w0b_sb[part, 0, :],
                                        ALU.add).then_inc(w0_ready, 1)
            nc.vector.tensor_tensor(w0[:, 1:BLOCK, :], w0a_sb[:, 1:BLOCK, :], w0b_sb[:, 1:BLOCK, :],
                                    ALU.add).then_inc(w0_ready, 1)
            nc.vector.tensor_tensor(w0m[MID_HH, :], w0ma_sb[MID_HH, :], w0mb_sb[MID_HH, :],
                                    ALU.add).then_inc(w0_ready, 1)
            nc.vector.memset(midfull[:, :], 0.0).then_inc(zeroed, 1)
            nc.vector.memset(midhigh[:, :].bitcast(fp32), 0.0).then_inc(zeroed, 1)
            nc.vector.memset(wmid[:, :].bitcast(fp32), 0.0).then_inc(zeroed, 1)
            dve.wait_ge(high_weights, 1)
            nc.vector.tensor_tensor(wmid[MID_LH, :], w0m[MID_HH, :], wmid[MID_HH, :],
                                    ALU.subtract).then_inc(low_weights, 1)
            for n in (1, 2):
                dve.wait_ge(high_weights, 1 + n)
                nc.vector.tensor_tensor(wl[n][:, :, :], wraw[n], wh[n][:, :, :],
                                        ALU.subtract).then_inc(low_weights, 1)

            def twice(t):
                return t.unsqueeze(1).to_broadcast([128, PAIR, COLS])

            def make(layer, c, s, g):
                kind, n, k = KIND[g], number(layer, c, g), slot(layer, c, g)
                if kind == "W":
                    wait(dve, used["W"], n - WRING + 1)
                    dst = whole[k][:, :, :]
                elif kind == "P":
                    wait(dve, low["P"], n - PRING + 1)
                    dst = pfull[:, k, :, :]
                else:
                    wait(dve, low["D"], n)
                    dst = dfull
                nc.vector.tensor_tensor(dst, xsh[s][:, g * PAIR:(g + 1) * PAIR, :],
                                        twice(h1 if layer == 1 else h2), ALU.mult
                                        ).then_inc(made[kind], 1)

            def take_low(layer, c, g):
                n, k = number(layer, c, g), slot(layer, c, g)
                dve.wait_ge(high["D"], n + 1)
                wait(dve, used["D"], n - DRING + 1)
                nc.vector.tensor_tensor(dlow[k][:, :, :], dfull, dhigh[k][:, :, :],
                                        ALU.subtract).then_inc(low["D"], 1)

            def layer0(c, s, i):
                dve.wait_ge(xps_ready, c + 1)
                dve.wait_ge(xsh_loaded[s][MID // BLOCK], 16 * GROUPS * (i + 1))
                wait(dve, mid_low, c)
                if isinstance(c, int) and c == 0:
                    dve.wait_ge(zeroed, 3)
                nc.vector.tensor_tensor(midfull[MID_HL, :], xsh[s][MID_HH, MID, :], xps[MID_HH, :],
                                        ALU.mult).then_inc(mid_full, 1)
                dve.wait_ge(xsh_loaded[s][0], 16 * GROUPS * (i + 1))
                for g in range(L0_PAIRS):
                    n = whole0(c, g)
                    wait(dve, used["W"], n - WRING + 1)
                    nc.vector.tensor_tensor(whole[slot0(c, g)][:, :, :],
                                            xsh[s][:, g * PAIR:(g + 1) * PAIR, :], twice(xps),
                                            ALU.mult).then_inc(made["W"], 1)

            def pool_kept2(c, s):
                dve.wait_ge(kept2_ready, c + 1)
                nc.vector.tensor_reduce(pool2[:, bass.ds(c * SAMPLES, SAMPLES)],
                                        kept2[s][:, :].rearrange("p (b e) -> p b e", e=EMBED),
                                        axis=AX.X, op=ALU.add).then_inc(pooled2, 1)

            def pool_kept01(c, s):
                dve.wait_ge(kept0_ready, c + 1)
                dve.wait_ge(kept1_ready, c + 1)
                nc.vector.tensor_reduce(pool01[:, bass.ds(c * SAMPLES, SAMPLES)],
                                        kept01[s][:, :].rearrange("p (b e) -> p b e", e=EMBED),
                                        axis=AX.X, op=ALU.add).then_inc(pooled01, 1)

            def chunk(c, s, i, first=False, last=False):
                for layer, h_ready in ((1, h1_ready), (2, h2_ready)):
                    dve.wait_ge(h_ready, c + 1)
                    for step in MAKE:
                        if isinstance(step, tuple):
                            take_low(layer, c, step[1])
                            continue
                        if layer == 1 and step % (BLOCK // PAIR) == 0:
                            dve.wait_ge(xsh_loaded[s][step * PAIR // BLOCK], 16 * GROUPS * (i + 1))
                        make(layer, c, s, step)
                    if layer == 1 and not last:
                        layer0(c + 1, 1 - s, i + s)
                    if layer == 1 and not first:
                        pool_kept2(c - 1, 1 - s)
                        pool_kept01(c - 1, 1 - s)

            layer0(0, 0, 0)
            for s in range(2):
                chunk(s, s, 0, first=s == 0)
            with dve.Fori(1, CHUNKS // 2 - 1) as i:
                for s in range(2):
                    chunk(2 * i + s, s, i)
            for s in range(2):
                chunk(CHUNKS - 2 + s, s, CHUNKS // 2 - 1, last=s == 1)
            pool_kept01(CHUNKS - 1, 1)
            pool_kept2(CHUNKS - 1, 1)

        @block.tensor
        def _(pe):
            def contract(layer, c, y):
                for g in USE:
                    kind, n, k = KIND[g], number(layer, c, g), slot(layer, c, g)
                    start, stop = g == USE[0], g == USE[-1]
                    if kind == "W":
                        pe.wait_ge(made["W"], n + 1)
                        j = ORDER["W"].index(g) * PAIR
                        terms = [(ww[layer][:, j + t, :], whole[k][:, t, :]) for t in range(PAIR)]
                    else:
                        pe.wait_ge(low[kind], n + 1)
                        j = SPLIT.index(g) * PAIR
                        zh, zl = (phigh, plow) if kind == "P" else (dhigh, dlow)
                        terms = []
                        for t in range(PAIR):
                            terms += [(wh[layer][:, j + t, :], zh[k][:, t, :]),
                                      (wh[layer][:, j + t, :], zl[k][:, t, :]),
                                      (wl[layer][:, j + t, :], zh[k][:, t, :])]
                    for m, (w, z) in enumerate(terms):
                        last = nc.tensor.matmul(y, w, z, start=start and m == 0,
                                                stop=stop and m == len(terms) - 1)
                    last.then_inc(used[kind], 1)

            def layer0(c):
                wait(pe, kept0_ready, c)
                for g in range(L0_PAIRS):
                    pe.wait_ge(made["W"], whole0(c, g) + 1)
                    for t in range(PAIR):
                        last = nc.tensor.matmul(y0, w0[:, g * PAIR + t, :], whole[slot0(c, g)][:, t, :],
                                                start=g == 0 and t == 0, stop=False)
                    last.then_inc(used["W"], 1)
                pe.wait_ge(mid_low, c + 1)
                nc.tensor.matmul(y0, wmid[:, :], zmid[:, :], start=False, stop=True
                                 ).then_inc(y0_ready, 1)

            def chunk(c, last=False):
                wait(pe, kept1_ready, c)
                contract(1, c, y1)
                if not last:
                    layer0(c + 1)
                wait(pe, kept2_ready, c)
                contract(2, c, y2)

            pe.wait_ge(w0_ready, GROUPS + 2)
            pe.wait_ge(low_weights, 1)
            layer0(0)
            pe.wait_ge(w12_loaded, 2 * 16)
            pe.wait_ge(low_weights, 3)
            for c in range(2):
                chunk(c)
            with pe.Fori(1, CHUNKS // 2 - 1) as i:
                for s in range(2):
                    chunk(2 * i + s)
            for s in range(2):
                chunk(CHUNKS - 2 + s, last=s == 1)

            pe.wait_ge(top_loaded, TOP_LOADS * 16)
            pe.wait_ge(pooled01, CHUNKS)
            pe.wait_ge(pooled2, CHUNKS)
            for n in range(2):
                cols = slice(n * COLS, (n + 1) * COLS)
                for m in range(HID1 // 128):
                    maps = slice(m * 128, (m + 1) * 128)
                    bank = banks[:, n * 4 + m, :]
                    nc.tensor.matmul(bank, wt1_sb[:, 0, maps], pool01[:, cols], start=True, stop=False)
                    nc.tensor.matmul(bank, wt1_sb[:, 1, maps], pool2[:, cols], start=False, stop=False)
                    nc.tensor.matmul(bank, wt1d_sb[:, maps], dense_sb[:, cols],
                                     start=False, stop=True).then_inc(hid1_psum, 1)
            for n in range(2):
                cols = slice(n * COLS, (n + 1) * COLS)
                pe.wait_ge(hid1_ready, (n + 1) * (HID1 // 128))
                for m in range(HID2 // 128):
                    for k in range(HID1 // 128):
                        last = nc.tensor.matmul(banks[:, n * 2 + m, :],
                                                wt2_sb[:, k, m * 128:(m + 1) * 128], hid1[:, k, cols],
                                                start=k == 0, stop=k == HID1 // 128 - 1)
                    last.then_inc(hid2_psum, 1)
            for n in range(2):
                cols = slice(n * COLS, (n + 1) * COLS)
                pe.wait_ge(hid2_ready, (n + 1) * (HID2 // 128))
                for k in range(HID2 // 128):
                    last = nc.tensor.matmul(banks[0:1, 4 + n, :], wt3_sb[:, k:k + 1], hid2[:, k, cols],
                                            start=k == 0, stop=k == HID2 // 128 - 1)
                last.then_inc(y_psum, 1)


def kernel(**inputs):
    import numpy as np
    import concourse.bacc as bacc
    from concourse.bass_utils import run_bass_kernel_spmd

    a = {k: np.asarray(v) for k, v in inputs.items()}
    tables = [a[f"tbl_{f}"] for f in range(FIELDS)]
    first_row = np.cumsum([0] + [t.shape[0] for t in tables[:-1]])
    ids = a["ids"].reshape(CHUNKS, GROUPS, PER_GROUP, FIELDS).transpose(1, 3, 0, 2)

    p = np.arange(128)[:, None]
    shifts = np.array([[shift(k, q) for k in range(TILES)] for q in range(GROUPS)])[p[:, 0] // FIELDS]
    field = (p % FIELDS + shifts) % FIELDS
    w0 = a["L0_rec_W0"].reshape(MAPS, FIELDS, FIELDS)
    own, other = np.broadcast_to(p % FIELDS, (128, BLOCK)), field[:, :BLOCK]
    mid = np.arange(MIDN)
    w1 = a["L0_rec_W1"].reshape(MAPS, FIELDS, HALF)
    w2 = a["L0_rec_W2"].reshape(MAPS, FIELDS, HALF)
    swap = np.r_[HALF:MAPS, 0:HALF]
    w1 = w1[swap][:, field, p % HALF].transpose(1, 2, 0)
    w2 = w2[:, field, p % HALF].transpose(1, 2, 0)
    whole_tiles = [g * PAIR + t for g in ORDER["W"] for t in range(PAIR)]
    split_tiles = [g * PAIR + t for g in SPLIT for t in range(PAIR)]
    arrays = {
        "tables": np.concatenate(tables, axis=0),
        "ids": ids.reshape(128, CHUNKS * PER_GROUP),
        "field_base": np.tile(first_row, GROUPS).astype(np.float32)[:, None],
        "dense_t": a["dense_ctx"].T,
        "w0a": w0[:, own, other].transpose(1, 2, 0),
        "w0b": w0[:, other, own].transpose(1, 2, 0),
        "w0ma": w0[:, mid, mid + MIDN].T,
        "w0mb": w0[:, mid + MIDN, mid].T,
        "w1_whole": w1[:, whole_tiles],
        "w1_split": w1[:, split_tiles],
        "w2_whole": w2[:, whole_tiles],
        "w2_split": w2[:, split_tiles],
        "bias0": a["L0_rec_b0"][:, None],
        "bias1": a["L0_rec_b1"][swap][:, None],
        "bias2": a["L0_rec_b2"][:, None],
        "wt1": a["W_top1"],
        "bt1": a["b_top1"].reshape(HID1 // 128, 128).T,
        "wt2": a["W_top2"],
        "bt2": a["b_top2"].reshape(HID2 // 128, 128).T,
        "wt3": a["W_top3"].reshape(HID2 // 128, 128).T,
    }
    nc = bacc.Bacc("TRN2", target_bir_lowering=False, num_devices=1)
    arrays = {f"in_{k}": np.ascontiguousarray(v) for k, v in arrays.items()}
    args = [nc.dram_tensor(k, v.shape, mybir.dt.from_np(v.dtype), kind="ExternalInput").ap()
            for k, v in arrays.items()]
    args.append(nc.dram_tensor("out_y", (BATCH, 1), mybir.dt.float32, kind="ExternalOutput").ap())
    dlrm_tower(nc, *args)
    return run_bass_kernel_spmd(nc, [arrays], core_ids=[0]).results[0]["out_y"]
```

```python
import concourse.bass as bass
from concourse import mybir
from contextlib import ExitStack

FIELDS = 32
EMBED = 16
BATCH = 1024
MAPS = 128
HALF = MAPS // 2
GROUPS = 4
SAMPLES = 32
CHUNKS = BATCH // SAMPLES
COLS = SAMPLES * EMBED
PER_GROUP = SAMPLES // GROUPS
TILES = FIELDS * HALF // 128
BLOCK = 4
BLOCKS = TILES // BLOCK
PAIR = 2
PAIRS = TILES // PAIR
STEP = 8
SHIFTS = [[0, 8, 12, 16], [8, 16, 20, 24], [4, 20, 24, 28], [12, 28, 32, 36]]
assert all(SHIFTS[q + 1][b] == SHIFTS[q][b] + STEP for q in (0, 2) for b in range(BLOCKS))
MID = BLOCK
MIDN = FIELDS // 2
MID_HH, MID_LH, MID_HL = (slice(q * FIELDS, q * FIELDS + MIDN) for q in (1, 2, 3))
COPIES = 3
ROWS = COPIES * FIELDS
DENSE = 16
HID1, HID2 = 512, 256
BLOCKS1, BLOCKS2 = HID1 // 128, HID2 // 128
PARTS = 3
DENSE_LH, DENSE_HL = slice(0, DENSE), slice((PARTS - 1) * DENSE, PARTS * DENSE)
EARLY = 3
LOADED = 16 * 2
TOP_LOADS = 7

KIND = ["P", "W", "D", "P", "W", "D", "P", "W"]
ORDER = {k: [g for g in range(PAIRS) if KIND[g] == k] for k in "WPD"}
MAKE = {1: [0, 1, 2, 3, ("low", 2), 4, 5, 6, 7, ("low", 5)],
        2: [2, 1, 0, 3, ("low", 2), 4, 5, 6, ("low", 5)]}
USE = {1: [1, 0, 2, 4, 3, 7, 5, 6],
       2: [1, 2, 0, 4, 3, 5, 6]}
TAIL = 7
assert TAIL == ORDER["W"][-1] and TAIL not in MAKE[2] + USE[2]
SPLIT = [g for g in range(PAIRS) if KIND[g] != "W"]
L0_PAIRS = 2
NW, NP, ND = (len(ORDER[k]) for k in "WPD")
WRING, PRING, DRING = 4, 3, 2
W_CHUNK = 2 * NW + L0_PAIRS
assert W_CHUNK % WRING == 0 and 2 * NP % PRING == 0 and 2 * ND % DRING == 0


def shift(k, quarter):
    return SHIFTS[quarter][k // BLOCK] + k % BLOCK


def in_block(g):
    return g * PAIR // BLOCK


def last_made(layer, block=None):
    order = MAKE[1] if layer == 1 else MAKE[2] + [TAIL]
    return [g for g in order if not isinstance(g, tuple) and block in (None, in_block(g))][-1]


def last_made_before_tail():
    return [g for g in MAKE[2] if not isinstance(g, tuple)][-1]


def first_of_block(layer, g):
    return [h for h in MAKE[layer] if not isinstance(h, tuple) and in_block(h) == in_block(g)][0] == g


def split_in_order(layer):
    return [g for g in MAKE[layer] if g in SPLIT]


def is_last(c):
    return isinstance(c, int) and c == CHUNKS - 1


def is_first(c):
    return isinstance(c, int) and c == 0


def whole0(c, g):
    return g if is_first(c) else L0_PAIRS - 1 + W_CHUNK * (c - 1) + NW + 1 + g


def number(layer, c, g):
    kind, j = KIND[g], ORDER[KIND[g]].index(g)
    if kind == "W":
        start = L0_PAIRS - 1 + W_CHUNK * c
        if layer == 1:
            return start + j + (1 if is_first(c) else 0)
        if g == TAIL and not is_last(c):
            return start + W_CHUNK + NW
        return start + NW + 1 + (0 if is_last(c) else L0_PAIRS) + j
    n = NP if kind == "P" else ND
    return 2 * n * c + (layer - 1) * n + j


def slot0(c, g):
    return whole0(0 if is_first(c) else 1, g) % WRING


def slot(layer, c, g):
    kind = KIND[g]
    alike = c if is_first(c) or is_last(c) else 1
    return number(layer, alike, g) % {"W": WRING, "P": PRING, "D": DRING}[kind]


def wait(eng, semaphore, count):
    if not (isinstance(count, int) and count < 1):
        eng.wait_ge(semaphore, count)


def dlrm_tower(nc, tables, ids, field_base, dense_t, w0a, w0b, w0ma, w0mb,
               w1_whole, w1_split, w2_whole, w2_split,
               bias0, bias1, bias2, wt1, bt1, wt2, bt2, wt3, out):
    fp32 = mybir.dt.float32
    fp32r = mybir.dt.float32r
    i32 = mybir.dt.int32
    ALU = mybir.AluOpType
    ACT = mybir.ActivationFunctionType
    AX = mybir.AxisListType

    ctx = ExitStack()
    with ctx:
        def sb(name, shape, dt=fp32):
            return ctx.enter_context(nc.sbuf_tensor(name, shape, dt))

        def sem(name):
            return ctx.enter_context(nc.semaphore(name))

        scratch = nc.dram_tensor("x_scratch", [CHUNKS, ROWS, COLS], fp32, kind="Internal")

        ids_sb = sb("ids_sb", [128, CHUNKS * PER_GROUP], i32)
        base_sb = sb("base_sb", [128, 1])
        rows_sb = sb("rows_sb", [128, CHUNKS * PER_GROUP], i32)
        rows_now = [sb(f"rows_now{s}", [128, PER_GROUP], i32) for s in range(2)]
        gathered = [sb(f"gathered{s}", [128, PER_GROUP * EMBED]) for s in range(2)]
        xsh, xsh_at = [], []
        for s in range(2):
            xsh.append(sb(f"xsh{s}", [128, TILES, COLS]))
            xsh_at.append(nc.sbuf_base - TILES * COLS * 4)
        xall = [sb(f"xall{s}", [128, COLS]) for s in range(2)]
        whole = [sb(f"whole{s}", [128, PAIR, COLS]) for s in range(WRING)]
        pfull = sb("pfull", [128, PRING, PAIR, COLS])
        phigh = [sb(f"phigh{s}", [128, PAIR, COLS], fp32r) for s in range(PRING)]
        plow = [sb(f"plow{s}", [128, PAIR, COLS], fp32r) for s in range(PRING)]
        dhigh = [sb(f"dhigh{s}", [128, PAIR, COLS], fp32r) for s in range(DRING)]
        dlow = [sb(f"dlow{s}", [128, PAIR, COLS], fp32r) for s in range(DRING)]
        midfull = sb("midfull", [128, COLS])
        midhigh = sb("midhigh", [128, COLS], fp32r)
        zmid = sb("zmid", [128, COLS], fp32r)
        kept01 = [sb(f"kept01{s}", [128, COLS]) for s in range(2)]
        kept2 = [sb(f"kept2{s}", [128, COLS]) for s in range(2)]
        pool01 = sb("pool01", [128, BATCH])
        pool2 = sb("pool2", [128, BATCH])
        w0ma_sb = sb("w0ma_sb", [128, MAPS])
        w0mb_sb = sb("w0mb_sb", [128, MAPS])
        w0 = sb("w0", [128, BLOCK, MAPS])
        w0m = sb("w0m", [128, MAPS])
        wmid = sb("wmid", [128, MAPS], fp32r)
        ww = {n: sb(f"w{n}_whole", [128, PAIR * NW, MAPS]) for n in (1, 2)}
        wh = {n: sb(f"w{n}_high", [128, PAIR * len(SPLIT), MAPS], fp32r) for n in (1, 2)}
        wl = {n: sb(f"w{n}_low", [128, PAIR * len(SPLIT), MAPS], fp32r) for n in (1, 2)}
        bias = [sb(f"bias{n}_sb", [128, 1]) for n in range(3)]
        wt1_sb = sb("wt1_sb", [128, 2, HID1])
        wt1d_sb = sb("wt1d_sb", [PARTS * DENSE, HID1])
        dense_sb = sb("dense_sb", [PARTS * DENSE, BATCH])
        bt1_sb = sb("bt1_sb", [128, HID1 // 128])
        wt2_sb = sb("wt2_sb", [128, HID1 // 128, HID2])
        bt2_sb = sb("bt2_sb", [128, HID2 // 128])
        wt3_sb = sb("wt3_sb", [128, HID2 // 128])
        parts = [nc.alloc_sbuf_tensor_at(f"parts{s}", [128, n, COLS], fp32r, offset=xsh_at[s])
                 for s, n in enumerate((15, 4))]

        def spare(s, first, tiles):
            return parts[s][:, first:first + tiles, :]

        wt1_high, wt1_low = spare(0, 0, 2), spare(0, 2, 2)
        wt2_high, wt2_low = (spare(0, t, 2).rearrange("p t (v j) -> p (t v) j", v=2)
                             for t in (4, 6))
        dense_parts = spare(0, 8, 2).rearrange("p t n -> p (t n)")[0:PARTS * DENSE, :]
        wt1d_parts = spare(0, 10, 1)[0:PARTS * DENSE, 0, :]
        pool_high, pool_low = ([spare(0, t, 2), spare(1, t - 11, 2)] for t in (11, 13))
        hid2 = xsh[1][:, 12:12 + 2 * BLOCKS2, :].rearrange("p (m h) n -> p m (h n)", h=2)
        hid1_full = pfull[:, :, :, :].rearrange("p s t n -> p (s t) n")
        FULL_RING = PAIR * PRING
        hid1_high = [[dhigh[m // PAIR][:, m % PAIR, :] for m in range(BLOCKS1)],
                     [phigh[m // PAIR][:, m % PAIR, :] for m in range(BLOCKS1)]]
        hid1_low = [[dlow[m // PAIR][:, m % PAIR, :] for m in range(BLOCKS1)],
                    [plow[m // PAIR][:, m % PAIR, :] for m in range(BLOCKS1)]]
        flat = pfull[:, :, :, :].rearrange("p s t n -> p (s t n)")
        n_split = PAIR * len(SPLIT) * MAPS
        wraw = {n: flat[:, (n - 1) * n_split:n * n_split].rearrange("p (t m) -> p t m", m=MAPS)
                for n in (1, 2)}
        w0a_sb = whole[2][:, 0, :].rearrange("p (t m) -> p t m", m=MAPS)
        w0b_sb = whole[2][:, 1, :].rearrange("p (t m) -> p t m", m=MAPS)
        y_sb = whole[3][0:1, :, :].rearrange("p t n -> p (t n)")

        banks = ctx.enter_context(nc.psum_tensor("banks", [128, 8, COLS], fp32))
        y0, y1, y2 = (banks[:, n, :] for n in range(3))
        h1, h2 = (banks[:, n, :] for n in range(3, 5))
        xps = banks[:, 5, :]
        dfull = banks[:, 6:8, :]
        HID1_BANKS = [[0, 3, 5, 1], [6, 7, 4, 2]]
        HID2_BANKS = [[0, 3], [5, 1]]
        Y_BANKS = [6, 7]

        ids_loaded = sem("ids_loaded")
        rows_ready = sem("rows_ready")
        rows_staged = sem("rows_staged")
        gather_done = [sem(f"gather_done{s}") for s in range(2)]
        scratch_written = [sem(f"scratch_written{s}") for s in range(2)]
        xall_loaded = [sem(f"xall_loaded{s}") for s in range(2)]
        xsh_loaded = [[sem(f"xsh_loaded{s}_{b}") for b in range(BLOCKS)] for s in range(2)]
        w0_loaded = sem("w0_loaded")
        w12_loaded = sem("w12_loaded")
        bias_loaded = sem("bias_loaded")
        top_loaded = sem("top_loaded")
        w0_ready = sem("w0_ready")
        weights_staged = sem("weights_staged")
        high_weights = sem("high_weights")
        low_weights = sem("low_weights")
        xps_ready = sem("xps_ready")
        made = {k: sem(f"made_{k}") for k in "WPD"}
        high = {k: sem(f"high_{k}") for k in "PD"}
        low = {k: sem(f"low_{k}") for k in "PD"}
        used = {k: sem(f"used_{k}") for k in "WPD"}
        zeroed = sem("zeroed")
        mid_full = sem("mid_full")
        mid_rounded = sem("mid_rounded")
        mid_high = sem("mid_high")
        mid_low = sem("mid_low")
        y0_ready = sem("y0_ready")
        h1_ready = sem("h1_ready")
        h2_ready = sem("h2_ready")
        kept0_ready = sem("kept0_ready")
        kept1_ready = sem("kept1_ready")
        kept2_ready = sem("kept2_ready")
        pooled01 = sem("pooled01")
        pooled2 = sem("pooled2")
        top_high = sem("top_high")
        top_low = sem("top_low")
        hid1_psum = sem("hid1_psum")
        hid1_rounded = sem("hid1_rounded")
        hid1_ready = sem("hid1_ready")
        hid2_psum = sem("hid2_psum")
        hid2_ready = sem("hid2_ready")
        y_psum = sem("y_psum")
        y_ready = sem("y_ready")
        y_stored = sem("y_stored")

        def shifted_rows(first):
            return bass.AP(tensor=scratch, offset=first * COLS,
                           ap=[[ROWS * COLS, CHUNKS], [STEP * COLS, 2],
                               [COLS, FIELDS], [1, BLOCK * COLS]])

        every_quarter = bass.AP(tensor=scratch, offset=0,
                                ap=[[ROWS * COLS, CHUNKS], [0, GROUPS], [COLS, FIELDS], [1, COLS]])

        block = ctx.enter_context(nc.Block())

        def all_copies(j):
            return bass.AP(tensor=scratch, offset=j * PER_GROUP * EMBED,
                           ap=[[ROWS * COLS, CHUNKS], [COLS, FIELDS], [FIELDS * COLS, COPIES],
                               [1, PER_GROUP * EMBED]])

        def pools(n, a, b):
            return [(x[:, n * COLS + a:n * COLS + b], pool_high[n][:, t, a:b], pool_low[n][:, t, a:b],
                     slice(0, 128)) for t, x in enumerate((pool01, pool2))]

        TOP_SPLITS = {
            "dense": [(dense_sb[:, :], dense_parts, dense_parts, DENSE_HL)],
            "wt1d": [(wt1d_sb[:, :], wt1d_parts, wt1d_parts, DENSE_LH)],
            "wt1": [(wt1_sb[:, :, :], wt1_high, wt1_low, slice(0, 128))],
            "pool of half 0": pools(0, 0, COLS),
            "wt2": [(wt2_sb[:, :, :], wt2_high, wt2_low, slice(0, 128))],
            "pool of half 1": pools(1, 0, COLS - SAMPLES),
            "pool of the last chunk": pools(1, COLS - SAMPLES, COLS),
        }

        def splits_done(name):
            return list(TOP_SPLITS).index(name) + 1

        def out_ready(eng, layer, c):
            g = USE[1][-1] if layer == 1 else TAIL
            eng.wait_ge(used[KIND[g]], number(layer, c, g) + 1)

        @block.sync
        def _(sp):
            sp.dma_start(ids_sb[:, :], ids).then_inc(ids_loaded, 16)

            def feed(c, s, i, first=False):
                sp.wait_ge(gather_done[s], 16 * PER_GROUP * (i + 1))
                for j in range(GROUPS):
                    sp.dma_start(
                        all_copies(j)[c],
                        gathered[s][j * FIELDS:(j + 1) * FIELDS, :].unsqueeze(1)
                        .to_broadcast([FIELDS, COPIES, PER_GROUP * EMBED]),
                    ).then_inc(scratch_written[s], 16)
                sp.wait_ge(scratch_written[s], 16 * GROUPS * (i + 1))
                for b in range(BLOCKS):
                    if not first:
                        g = last_made(2, b)
                        sp.wait_ge(made[KIND[g]], number(2, c - 2, g) + 1)
                    if b == 0:
                        sp.dma_start(xall[s][:, :], every_quarter[c]).then_inc(xall_loaded[s], 16)
                    for q in range(0, GROUPS, 2):
                        sp.dma_start(
                            xsh[s][q * FIELDS:(q + 2) * FIELDS, b * BLOCK:(b + 1) * BLOCK, :],
                            shifted_rows(SHIFTS[q][b])[c],
                        ).then_inc(xsh_loaded[s][b], 16)

            for s in range(2):
                feed(s, s, 0, first=True)
            top = [(wt1_sb[:, :, :], wt1[0:2 * 128, :].rearrange("(t p) n -> p t n", p=128)),
                   (wt1d_sb[:, :], wt1[2 * 128:2 * 128 + DENSE, :].unsqueeze(0)
                    .to_broadcast([PARTS, DENSE, HID1])),
                   (dense_sb[:, :], dense_t.unsqueeze(0).to_broadcast([PARTS, DENSE, BATCH])), (bt1_sb[:, :], bt1),
                   (wt2_sb[:, :, :], wt2.rearrange("(t p) n -> p t n", p=128)),
                   (bt2_sb[:, :], bt2), (wt3_sb[:, :], wt3)]
            for dst, src in top:
                sp.dma_start(dst, src).then_inc(top_loaded, 16)
            with sp.Fori(1, CHUNKS // 2) as i:
                for s in range(2):
                    feed(2 * i + s, s, i)
            sp.wait_ge(y_ready, 2)
            sp.dma_start(out.rearrange("b one -> one b"), y_sb).then_inc(y_stored, 16)
            sp.wait_ge(y_stored, 16)

        @block.gpsimd
        def _(pool):
            def stage_rows(c, s):
                nc.gpsimd.tensor_copy(rows_now[s][:, :], rows_sb[:, bass.ds(c * PER_GROUP, PER_GROUP)]
                                      ).then_inc(rows_staged, 1)
                pool.wait_ge(rows_staged, 1)
                pool.sem_inc(rows_staged, -1)

            def gather(s, n):
                pool.indirect_dma_start(
                    out=gathered[s][:, n * EMBED:(n + 1) * EMBED], out_offset=None,
                    in_=tables,
                    in_offset=bass.IndirectOffsetOnAxis(ap=rows_now[s][:, n:n + 1], axis=0),
                ).then_inc(gather_done[s], 16)

            def take_low(layer, c, g):
                n, k = number(layer, c, g), slot(layer, c, g)
                pool.wait_ge(high["P"], n + 1)
                wait(pool, used["P"], n - PRING + 1)
                nc.gpsimd.tensor_tensor(plow[k][:, :, :], pfull[:, k, :, :], phigh[k][:, :, :],
                                        ALU.subtract).then_inc(low["P"], 1)

            def take_mid_low(c):
                pool.wait_ge(mid_high, c + 1)
                wait(pool, y0_ready, c)
                nc.gpsimd.tensor_tensor(zmid[:, :], midfull[:, :], midhigh[:, :],
                                        ALU.subtract).then_inc(mid_low, 1)

            half = PER_GROUP // 2
            share = {1: [0, 0, 1, 2, 1], 2: [3, 0, 1, 0]}
            assert sum(share[1]) == sum(share[2]) == half

            def free_buffer(s, i):
                pool.wait_ge(scratch_written[s], 16 * GROUPS * (i + 1))

            def chunk(c, s, i):
                for layer, ahead, first in ((1, 2, half), (2, 3, 0)):
                    gathers = not (isinstance(c, int) and c + ahead >= CHUNKS)
                    to = s if ahead == 2 else 1 - s
                    if gathers and first == 0:
                        free_buffer(to, i + s)
                        stage_rows(c + ahead, to)
                    n = first
                    for j in range(len(share[layer])):
                        if j > NP:
                            if not is_last(c):
                                take_mid_low(c + 1)
                        elif j > 0:
                            take_low(layer, c, ORDER["P"][j - 1])
                        for _ in range(share[layer][j] if gathers else 0):
                            gather(to, n)
                            n += 1

            pool.wait_ge(rows_ready, 1)
            for s in range(2):
                stage_rows(s, s)
                for n in range(PER_GROUP):
                    gather(s, n)
            free_buffer(0, 0)
            stage_rows(2, 0)
            for n in range(half):
                gather(0, n)
            take_mid_low(0)
            for s in range(2):
                chunk(s, s, 0)
            with pool.Fori(1, CHUNKS // 2 - 2) as i:
                for s in range(2):
                    chunk(2 * i + s, s, i)
            for c in range(CHUNKS - 4, CHUNKS):
                chunk(c, c % 2, c // 2)

        @block.scalar
        def _(act):
            act.dma_start(base_sb[:, :], field_base).then_inc(ids_loaded, 16)
            act.dma_start(w0a_sb, w0a).then_inc(w0_loaded, 16)
            act.dma_start(w0b_sb, w0b).then_inc(w0_loaded, 16)
            act.dma_start(w0ma_sb[MID_HH, :], w0ma).then_inc(w0_loaded, 16)
            act.dma_start(w0mb_sb[MID_HH, :], w0mb).then_inc(w0_loaded, 16)
            for n, b in enumerate((bias0, bias1, bias2)):
                act.dma_start(bias[n][:, :], b).then_inc(bias_loaded, 16)
            for n, w in ((1, w1_split), (2, w2_split)):
                act.dma_start(wraw[n], w).then_inc(weights_staged, 16)
            for n, w in ((1, w1_whole), (2, w2_whole)):
                act.dma_start(ww[n][:, :, :], w).then_inc(w12_loaded, 16)
            act.wait_ge(w0_ready, GROUPS + 2)
            act.wait_ge(zeroed, 3)
            nc.scalar.copy(wmid[MID_HH, :], w0m[MID_HH, :])
            nc.scalar.copy(wmid[MID_HL, :], w0m[MID_HH, :]).then_inc(high_weights, 1)
            act.wait_ge(weights_staged, 2 * 16)
            for n in (1, 2):
                nc.scalar.copy(wh[n][:, :, :], wraw[n]).then_inc(high_weights, 1)
            act.wait_ge(bias_loaded, 3 * 16)

            def relu(dst, src, b):
                return nc.scalar.activation(dst, src, ACT.Relu, bias=b)

            def copy_x(c, s, i):
                act.wait_ge(xall_loaded[s], 16 * (i + 1))
                if not (isinstance(c, int) and c == 0):
                    act.wait_ge(made["W"], whole0(c - 1, L0_PAIRS - 1) + 1)
                nc.scalar.copy(xps, xall[s][:, :]).then_inc(xps_ready, 1)

            def take_high(layer, c, g):
                kind, n, k = KIND[g], number(layer, c, g), slot(layer, c, g)
                full = pfull[:, k, :, :] if kind == "P" else dfull
                act.wait_ge(made[kind], n + 1)
                wait(act, used[kind], n - (PRING if kind == "P" else DRING) + 1)
                nc.scalar.copy((phigh if kind == "P" else dhigh)[k][:, :, :], full
                               ).then_inc(high[kind], 1)

            def take_mid_high(c):
                act.wait_ge(mid_full, c + 1)
                nc.scalar.copy(midhigh[MID_HL, :], midfull[MID_HL, :]).then_inc(mid_rounded, 1)
                act.wait_ge(mid_rounded, c + 1)
                nc.scalar.copy(midfull[MID_LH, :], midhigh[MID_HL, :])
                nc.scalar.copy(midfull[MID_HH, :], midhigh[MID_HL, :]).then_inc(mid_high, 1)

            def after_layer0(c, s):
                act.wait_ge(y0_ready, c + 1)
                if not (isinstance(c, int) and c == 0):
                    g = last_made(1)
                    act.wait_ge(made[KIND[g]], number(1, c - 1, g) + 1)
                relu(h1[0:HALF, :], y0[HALF:MAPS, :], bias[0][HALF:MAPS, :])
                relu(h1[HALF:MAPS, :], y0[HALF:MAPS, :], bias[0][HALF:MAPS, :]).then_inc(h1_ready, 1)
                wait(act, pooled01, c - 1)
                relu(kept01[s][0:HALF, :], y0[0:HALF, :], bias[0][0:HALF, :]).then_inc(kept0_ready, 1)

            def after_layer2(c, s):
                out_ready(act, 2, c)
                wait(act, pooled2, c - 1)
                relu(kept2[s][:, :], y2, bias[2][:, :]).then_inc(kept2_ready, 1)

            def round_top(name):
                for x, high_part, _, _ in TOP_SPLITS[name]:
                    rounding = nc.scalar.copy(high_part, x)
                rounding.then_inc(top_high, 1)

            def hidden1(n, m):
                b = n * BLOCKS1 + m
                act.wait_ge(hid1_psum, b + 1)
                wait(act, hid1_ready, b - FULL_RING + 1)
                bank = banks[:, HID1_BANKS[n][m], :]
                relu(hid1_full[:, b % FULL_RING, :], bank, bt1_sb[:, m:m + 1])
                relu(hid1_high[n][m], bank, bt1_sb[:, m:m + 1]).then_inc(hid1_rounded, 1)

            def chunk(c, s, i, first=False, last=False):
                if last:
                    act.wait_ge(top_loaded, TOP_LOADS * 16)
                    g = last_made_before_tail()
                    act.wait_ge(made[KIND[g]], number(2, c - 1, g) + 1)
                    round_top("dense")
                split = split_in_order(1)
                take_high(1, c, split[0])
                if last:
                    round_top("wt1d")
                    round_top("wt1")
                if not last:
                    copy_x(c + 1, 1 - s, i + s)
                for g in split[1:3]:
                    take_high(1, c, g)
                if last:
                    act.wait_ge(pooled01, CHUNKS // 2)
                    act.wait_ge(pooled2, CHUNKS // 2)
                    round_top("pool of half 0")
                for g in split[3:]:
                    take_high(1, c, g)
                if not last:
                    take_mid_high(c + 1)
                out_ready(act, 1, c)
                if not first:
                    act.wait_ge(made["W"], number(2, c - 1, TAIL) + 1)
                relu(h2[0:HALF, :], y1[0:HALF, :], bias[1][0:HALF, :])
                relu(h2[HALF:MAPS, :], y1[0:HALF, :], bias[1][0:HALF, :]).then_inc(h2_ready, 1)
                split = split_in_order(2)
                relu(kept01[s][HALF:MAPS, :], y1[HALF:MAPS, :], bias[1][HALF:MAPS, :]
                     ).then_inc(kept1_ready, 1)
                if not first:
                    after_layer2(c - 1, 1 - s)
                for g in split[:3]:
                    take_high(2, c, g)
                if last:
                    round_top("wt2")
                if not last:
                    after_layer0(c + 1, 1 - s)
                for g in split[3:]:
                    take_high(2, c, g)

            copy_x(0, 0, 0)
            take_mid_high(0)
            after_layer0(0, 0)
            for s in range(2):
                chunk(s, s, 0, first=s == 0)
            with act.Fori(1, CHUNKS // 2 - 1) as i:
                for s in range(2):
                    chunk(2 * i + s, s, i)
            for s in range(2):
                chunk(CHUNKS - 2 + s, s, CHUNKS // 2 - 1, last=s == 1)
            g = last_made(2)
            act.wait_ge(made[KIND[g]], number(2, CHUNKS - 1, g) + 1)
            act.wait_ge(pooled01, CHUNKS - 1)
            act.wait_ge(pooled2, CHUNKS - 1)
            round_top("pool of half 1")
            after_layer2(CHUNKS - 1, 1)

            for n in range(2):
                for m in range(BLOCKS1):
                    if n == 0 and m == 1:
                        act.wait_ge(pooled01, CHUNKS)
                        act.wait_ge(pooled2, CHUNKS)
                        round_top("pool of the last chunk")
                    hidden1(n, m)
            for n in range(2):
                for m in range(BLOCKS2):
                    act.wait_ge(hid2_psum, n * BLOCKS2 + m + 1)
                    relu(hid2[:, m, n * COLS:(n + 1) * COLS], banks[:, HID2_BANKS[n][m], :],
                         bt2_sb[:, m:m + 1]).then_inc(hid2_ready, 1)
            for n in range(2):
                act.wait_ge(y_psum, n + 1)
                nc.scalar.copy(y_sb[:, n * COLS:(n + 1) * COLS], banks[0:1, Y_BANKS[n], :]).then_inc(y_ready, 1)

        @block.vector
        def _(dve):
            dve.wait_ge(ids_loaded, 2 * 16)
            nc.vector.tensor_scalar(rows_sb[:, :], ids_sb[:, :], base_sb[:, 0:1], None,
                                    ALU.add).then_inc(rows_ready, 1)
            dve.wait_ge(w0_loaded, 4 * 16)
            nc.vector.tensor_copy(w0[0:FIELDS, 0, :], w0a_sb[0:FIELDS, 0, :]).then_inc(w0_ready, 1)
            for q in range(1, GROUPS):
                part = slice(q * FIELDS, (q + 1) * FIELDS)
                nc.vector.tensor_tensor(w0[part, 0, :], w0a_sb[part, 0, :], w0b_sb[part, 0, :],
                                        ALU.add).then_inc(w0_ready, 1)
            nc.vector.tensor_tensor(w0[:, 1:BLOCK, :], w0a_sb[:, 1:BLOCK, :], w0b_sb[:, 1:BLOCK, :],
                                    ALU.add).then_inc(w0_ready, 1)
            nc.vector.tensor_tensor(w0m[MID_HH, :], w0ma_sb[MID_HH, :], w0mb_sb[MID_HH, :],
                                    ALU.add).then_inc(w0_ready, 1)
            nc.vector.memset(midfull[:, :], 0.0).then_inc(zeroed, 1)
            nc.vector.memset(midhigh[:, :].bitcast(fp32), 0.0).then_inc(zeroed, 1)
            nc.vector.memset(wmid[:, :].bitcast(fp32), 0.0).then_inc(zeroed, 1)
            dve.wait_ge(high_weights, 1)
            nc.vector.tensor_tensor(wmid[MID_LH, :], w0m[MID_HH, :], wmid[MID_HH, :],
                                    ALU.subtract).then_inc(low_weights, 1)
            for n in (1, 2):
                dve.wait_ge(high_weights, 1 + n)
                nc.vector.tensor_tensor(wl[n][:, :, :], wraw[n], wh[n][:, :, :],
                                        ALU.subtract).then_inc(low_weights, 1)

            def twice(t):
                return t.unsqueeze(1).to_broadcast([128, PAIR, COLS])

            def make(layer, c, s, g):
                kind, n, k = KIND[g], number(layer, c, g), slot(layer, c, g)
                if kind == "W":
                    wait(dve, used["W"], n - WRING + 1)
                    dst = whole[k][:, :, :]
                elif kind == "P":
                    wait(dve, low["P"], n - PRING + 1)
                    dst = pfull[:, k, :, :]
                else:
                    wait(dve, low["D"], n)
                    dst = dfull
                nc.vector.tensor_tensor(dst, xsh[s][:, g * PAIR:(g + 1) * PAIR, :],
                                        twice(h1 if layer == 1 else h2), ALU.mult
                                        ).then_inc(made[kind], 1)

            def take_low(layer, c, g):
                n, k = number(layer, c, g), slot(layer, c, g)
                dve.wait_ge(high["D"], n + 1)
                wait(dve, used["D"], n - DRING + 1)
                nc.vector.tensor_tensor(dlow[k][:, :, :], dfull, dhigh[k][:, :, :],
                                        ALU.subtract).then_inc(low["D"], 1)

            def layer0_mid(c, s, i):
                dve.wait_ge(xsh_loaded[s][MID // BLOCK], LOADED * (i + 1))
                wait(dve, mid_low, c)
                if isinstance(c, int) and c == 0:
                    dve.wait_ge(zeroed, 3)
                nc.vector.tensor_tensor(midfull[MID_HL, :], xsh[s][MID_HH, MID, :], xps[MID_HH, :],
                                        ALU.mult).then_inc(mid_full, 1)

            def layer0(c, s, i):
                at_start = isinstance(c, int) and c == 0
                dve.wait_ge(xps_ready, c + 1)
                if not at_start:
                    layer0_mid(c, s, i)
                dve.wait_ge(xsh_loaded[s][0], LOADED * (i + 1))
                for g in range(L0_PAIRS):
                    n = whole0(c, g)
                    wait(dve, used["W"], n - WRING + 1)
                    nc.vector.tensor_tensor(whole[slot0(c, g)][:, :, :],
                                            xsh[s][:, g * PAIR:(g + 1) * PAIR, :], twice(xps),
                                            ALU.mult).then_inc(made["W"], 1)
                if at_start:
                    layer0_mid(c, s, i)

            def pool_kept2(c, s):
                dve.wait_ge(kept2_ready, c + 1)
                nc.vector.tensor_reduce(pool2[:, bass.ds(c * SAMPLES, SAMPLES)],
                                        kept2[s][:, :].rearrange("p (b e) -> p b e", e=EMBED),
                                        axis=AX.X, op=ALU.add).then_inc(pooled2, 1)

            def pool_kept01(c, s):
                dve.wait_ge(kept0_ready, c + 1)
                dve.wait_ge(kept1_ready, c + 1)
                nc.vector.tensor_reduce(pool01[:, bass.ds(c * SAMPLES, SAMPLES)],
                                        kept01[s][:, :].rearrange("p (b e) -> p b e", e=EMBED),
                                        axis=AX.X, op=ALU.add).then_inc(pooled01, 1)

            def take_top_low(name):
                dve.wait_ge(top_high, splits_done(name))
                for x, high_part, low_part, rows in TOP_SPLITS[name]:
                    taking = nc.vector.tensor_tensor(low_part[rows], x[rows], high_part[rows],
                                                     ALU.subtract)
                taking.then_inc(top_low, 1)

            def hidden1_low(n, m):
                b = n * BLOCKS1 + m
                dve.wait_ge(hid1_rounded, b + 1)
                nc.vector.tensor_tensor(hid1_low[n][m], hid1_full[:, b % FULL_RING, :],
                                        hid1_high[n][m], ALU.subtract).then_inc(hid1_ready, 1)

            def chunk(c, s, i, first=False, last=False):
                for layer, h_ready in ((1, h1_ready), (2, h2_ready)):
                    dve.wait_ge(h_ready, c + 1)
                    for step in MAKE[layer]:
                        if isinstance(step, tuple):
                            take_low(layer, c, step[1])
                            continue
                        if layer == 1 and first_of_block(1, step):
                            dve.wait_ge(xsh_loaded[s][in_block(step)], LOADED * (i + 1))
                        make(layer, c, s, step)
                    if layer == 1 and not first:
                        make(2, c - 1, 1 - s, TAIL)
                    if layer == 1 and not last:
                        layer0(c + 1, 1 - s, i + s)
                    if layer == 1 and not first and not last:
                        pool_kept01(c - 1, 1 - s)
                        if not (isinstance(c, int) and c < 2):
                            pool_kept2(c - 2, s)
                    if layer == 1 and last:
                        dve.wait_ge(made["W"], number(2, c - 1, TAIL) + 1)
                        for name in ("dense", "wt1d", "wt1", "pool of half 0"):
                            take_top_low(name)

            layer0(0, 0, 0)
            for s in range(2):
                chunk(s, s, 0, first=s == 0)
            with dve.Fori(1, CHUNKS // 2 - 1) as i:
                for s in range(2):
                    chunk(2 * i + s, s, i)
            for s in range(2):
                chunk(CHUNKS - 2 + s, s, CHUNKS // 2 - 1, last=s == 1)
            make(2, CHUNKS - 1, 1, TAIL)
            pool_kept2(CHUNKS - 3, 1)
            pool_kept2(CHUNKS - 2, 0)
            pool_kept01(CHUNKS - 2, 0)
            take_top_low("wt2")
            take_top_low("pool of half 1")
            pool_kept01(CHUNKS - 1, 1)
            pool_kept2(CHUNKS - 1, 1)
            take_top_low("pool of the last chunk")
            for n in range(2):
                for m in range(BLOCKS1):
                    hidden1_low(n, m)

        @block.tensor
        def _(pe):
            def contract(layer, c, y, pairs):
                for g in pairs:
                    kind, n, k = KIND[g], number(layer, c, g), slot(layer, c, g)
                    start, stop = g == USE[layer][0], g == (USE[1][-1] if layer == 1 else TAIL)
                    if kind == "W":
                        pe.wait_ge(made["W"], n + 1)
                        j = ORDER["W"].index(g) * PAIR
                        terms = [(ww[layer][:, j + t, :], whole[k][:, t, :]) for t in range(PAIR)]
                    else:
                        pe.wait_ge(low[kind], n + 1)
                        j = SPLIT.index(g) * PAIR
                        zh, zl = (phigh, plow) if kind == "P" else (dhigh, dlow)
                        terms = []
                        for t in range(PAIR):
                            terms += [(wh[layer][:, j + t, :], zh[k][:, t, :]),
                                      (wh[layer][:, j + t, :], zl[k][:, t, :]),
                                      (wl[layer][:, j + t, :], zh[k][:, t, :])]
                    for m, (w, z) in enumerate(terms):
                        last = nc.tensor.matmul(y, w, z, start=start and m == 0,
                                                stop=stop and m == len(terms) - 1)
                    last.then_inc(used[kind], 1)

            def layer0(c):
                wait(pe, kept0_ready, c)
                for g in range(L0_PAIRS):
                    pe.wait_ge(made["W"], whole0(c, g) + 1)
                    for t in range(PAIR):
                        last = nc.tensor.matmul(y0, w0[:, g * PAIR + t, :], whole[slot0(c, g)][:, t, :],
                                                start=g == 0 and t == 0, stop=False)
                    last.then_inc(used["W"], 1)
                pe.wait_ge(mid_low, c + 1)
                nc.tensor.matmul(y0, wmid[:, :], zmid[:, :], start=False, stop=True
                                 ).then_inc(y0_ready, 1)

            def hidden1(n, m):
                maps, bank = slice(m * 128, (m + 1) * 128), banks[:, HID1_BANKS[n][m], :]
                for t in range(2):
                    for w, x in ((wt1_high, pool_high), (wt1_high, pool_low), (wt1_low, pool_high)):
                        nc.tensor.matmul(bank, w[:, t, maps], x[n][:, t, :],
                                         start=t == 0 and w is wt1_high and x is pool_high, stop=False)
                nc.tensor.matmul(bank, wt1d_parts[:, maps], dense_parts[:, n * COLS:(n + 1) * COLS],
                                 start=False, stop=True).then_inc(hid1_psum, 1)

            def chunk(c, first=False, last=False):
                wait(pe, kept1_ready, c)
                contract(1, c, y1, USE[1])
                if not first:
                    contract(2, c - 1, y2, [TAIL])
                if not last:
                    layer0(c + 1)
                else:
                    pe.wait_ge(top_low, splits_done("pool of half 0"))
                    pe.wait_ge(kept0_ready, CHUNKS)
                    for m in range(EARLY):
                        hidden1(0, m)
                wait(pe, kept2_ready, c)
                contract(2, c, y2, USE[2])

            pe.wait_ge(w0_ready, GROUPS + 2)
            pe.wait_ge(low_weights, 1)
            layer0(0)
            pe.wait_ge(w12_loaded, 2 * 16)
            pe.wait_ge(low_weights, 3)
            for c in range(2):
                chunk(c, first=c == 0)
            with pe.Fori(1, CHUNKS // 2 - 1) as i:
                for s in range(2):
                    chunk(2 * i + s)
            for s in range(2):
                chunk(CHUNKS - 2 + s, last=s == 1)

            contract(2, CHUNKS - 1, y2, [TAIL])

            pe.wait_ge(kept1_ready, CHUNKS)
            for m in range(EARLY, BLOCKS1):
                hidden1(0, m)
            pe.wait_ge(top_low, splits_done("pool of the last chunk"))
            for m in range(BLOCKS1):
                hidden1(1, m)
            for n in range(2):
                pe.wait_ge(hid1_ready, (n + 1) * BLOCKS1)
                for m in range(BLOCKS2):
                    maps, bank = slice(m * 128, (m + 1) * 128), banks[:, HID2_BANKS[n][m], :]
                    for k in range(BLOCKS1):
                        terms = [(wt2_high, hid1_high), (wt2_high, hid1_low), (wt2_low, hid1_high)]
                        for j, (w, x) in enumerate(terms):
                            last = nc.tensor.matmul(bank, w[:, k, maps], x[n][k],
                                                    start=k == 0 and j == 0,
                                                    stop=k == BLOCKS1 - 1 and j == PARTS - 1)
                    last.then_inc(hid2_psum, 1)
            for n in range(2):
                cols = slice(n * COLS, (n + 1) * COLS)
                pe.wait_ge(hid2_ready, (n + 1) * BLOCKS2)
                for k in range(BLOCKS2):
                    last = nc.tensor.matmul(banks[0:1, Y_BANKS[n], :], wt3_sb[:, k:k + 1], hid2[:, k, cols],
                                            start=k == 0, stop=k == BLOCKS2 - 1)
                last.then_inc(y_psum, 1)


def kernel(**inputs):
    import numpy as np
    import concourse.bacc as bacc
    from concourse.bass_utils import run_bass_kernel_spmd

    a = {k: np.asarray(v) for k, v in inputs.items()}
    tables = [a[f"tbl_{f}"] for f in range(FIELDS)]
    first_row = np.cumsum([0] + [t.shape[0] for t in tables[:-1]])
    ids = a["ids"].reshape(CHUNKS, GROUPS, PER_GROUP, FIELDS).transpose(1, 3, 0, 2)

    p = np.arange(128)[:, None]
    shifts = np.array([[shift(k, q) for k in range(TILES)] for q in range(GROUPS)])[p[:, 0] // FIELDS]
    field = (p % FIELDS + shifts) % FIELDS
    w0 = a["L0_rec_W0"].reshape(MAPS, FIELDS, FIELDS)
    own, other = np.broadcast_to(p % FIELDS, (128, BLOCK)), field[:, :BLOCK]
    mid = np.arange(MIDN)
    w1 = a["L0_rec_W1"].reshape(MAPS, FIELDS, HALF)
    w2 = a["L0_rec_W2"].reshape(MAPS, FIELDS, HALF)
    swap = np.r_[HALF:MAPS, 0:HALF]
    w1 = w1[swap][:, field, p % HALF].transpose(1, 2, 0)
    w2 = w2[:, field, p % HALF].transpose(1, 2, 0)
    whole_tiles = [g * PAIR + t for g in ORDER["W"] for t in range(PAIR)]
    split_tiles = [g * PAIR + t for g in SPLIT for t in range(PAIR)]
    arrays = {
        "tables": np.concatenate(tables, axis=0),
        "ids": ids.reshape(128, CHUNKS * PER_GROUP),
        "field_base": np.tile(first_row, GROUPS).astype(np.float32)[:, None],
        "dense_t": a["dense_ctx"].T,
        "w0a": w0[:, own, other].transpose(1, 2, 0),
        "w0b": w0[:, other, own].transpose(1, 2, 0),
        "w0ma": w0[:, mid, mid + MIDN].T,
        "w0mb": w0[:, mid + MIDN, mid].T,
        "w1_whole": w1[:, whole_tiles],
        "w1_split": w1[:, split_tiles],
        "w2_whole": w2[:, whole_tiles],
        "w2_split": w2[:, split_tiles],
        "bias0": a["L0_rec_b0"][:, None],
        "bias1": a["L0_rec_b1"][swap][:, None],
        "bias2": a["L0_rec_b2"][:, None],
        "wt1": a["W_top1"],
        "bt1": a["b_top1"].reshape(HID1 // 128, 128).T,
        "wt2": a["W_top2"],
        "bt2": a["b_top2"].reshape(HID2 // 128, 128).T,
        "wt3": a["W_top3"].reshape(HID2 // 128, 128).T,
    }
    nc = bacc.Bacc("TRN2", target_bir_lowering=False, num_devices=1)
    arrays = {f"in_{k}": np.ascontiguousarray(v) for k, v in arrays.items()}
    args = [nc.dram_tensor(k, v.shape, mybir.dt.from_np(v.dtype), kind="ExternalInput").ap()
            for k, v in arrays.items()]
    args.append(nc.dram_tensor("out_y", (BATCH, 1), mybir.dt.float32, kind="ExternalOutput").ap())
    dlrm_tower(nc, *args)
    return run_bass_kernel_spmd(nc, [arrays], core_ids=[0]).results[0]["out_y"]
```
